# Optimizing a Trainium2 kernel written in Bass

```python
import numpy as np
import jax
import jax.numpy as jnp

def _softmax(x, axis=-1):
    return jax.nn.softmax(x, axis=axis)

def _gelu(x):
    return jax.nn.gelu(x, approximate=True)

def _silu(x):
    return jax.nn.silu(x)

def _sigmoid(x):
    return jax.nn.sigmoid(x)

def _layernorm(x, axis=-1, eps=1e-05):
    m = jnp.mean(x, axis=axis, keepdims=True)
    v = jnp.var(x, axis=axis, keepdims=True)
    return (x - m) / jnp.sqrt(v + eps)

def _scatter_add(tgt, idx, src, axis=0):
    return tgt.at[idx].add(src)

def _segment_sum(src, seg, n):
    return jax.ops.segment_sum(src, seg, n)
kernel_name = 'mk_adj_resnorm_d2_adj_r2_97ec63'

def setup_inputs(seed: int=0):
    np.random.seed(seed)
    _w = jnp.asarray

    def _rec_inputs():
        import jax
        import jax.numpy as jnp
        _gk = jax.random.key(seed)
        x = 7.22e-05 + 1 * jax.random.normal(jax.random.fold_in(_gk, 1), (4096, 512), jnp.float32)
        _w = (1.0 + jnp.arange(4096, dtype=jnp.float32)) ** (-0.5)
        _w = _w / _w.mean()
        _pij = jnp.clip(0.000488281 * _w[:, None] * _w[None, :], 0.0, 1.0)
        _a = jax.random.uniform(jax.random.fold_in(_gk, 2), (4096, 4096)) < _pij
        _af = _a.astype(jnp.float32)
        adj = _af
        return (x, adj)
    x, adj = _rec_inputs()

    def _L0_gnn_setup():
        import jax, jax.numpy as jnp
        import numpy as np
        N = 4096
        D = 512
        key = jax.random.key(seed)
        ks = jax.random.split(key, 13)
        w_scale = 1.0 / np.sqrt(D)
        inp = {'query': jax.random.normal(ks[0], (N, D), dtype=jnp.float32), 'key': jax.random.normal(ks[1], (N, D), dtype=jnp.float32), 'value': jax.random.normal(ks[2], (N, D), dtype=jnp.float32), 'adj_matrix': jax.random.randint(ks[3], (N, N), 0, 2).astype(jnp.float32), 'Wq': jax.random.normal(ks[4], (D, D), dtype=jnp.float32) * w_scale, 'bq': jax.random.normal(ks[5], (D,), dtype=jnp.float32) * 0.01, 'Wk': jax.random.normal(ks[6], (D, D), dtype=jnp.float32) * w_scale, 'bk': jax.random.normal(ks[7], (D,), dtype=jnp.float32) * 0.01, 'Wv': jax.random.normal(ks[8], (D, D), dtype=jnp.float32) * w_scale, 'bv': jax.random.normal(ks[9], (D,), dtype=jnp.float32) * 0.01, 'Wm': jax.random.normal(ks[10], (D, D), dtype=jnp.float32) * w_scale, 'bm': jax.random.normal(ks[11], (D,), dtype=jnp.float32) * 0.01}
        return inp
    _L0_gnn_all = _L0_gnn_setup()
    _L0_gnn_in = {k: v for k, v in _L0_gnn_all.items() if k in ('key', 'value', 'Wq', 'bq', 'Wk', 'bk', 'Wv', 'bv', 'Wm', 'bm')}
    del _L0_gnn_all

    def _L1_gnn_setup():
        import jax, jax.numpy as jnp
        import numpy as np
        N = 4096
        D_IN = 512
        D_OUT = 512
        key = jax.random.key(seed)
        k1, k2, k3, k4 = jax.random.split(key, 4)
        features = jax.random.normal(k1, (N, D_IN), dtype=jnp.float32)
        adj = jax.random.uniform(k2, (N, N), dtype=jnp.float32)
        W = jax.random.normal(k3, (D_OUT, D_IN), dtype=jnp.float32) * (1.0 / np.sqrt(D_IN))
        b = jax.random.normal(k4, (D_OUT,), dtype=jnp.float32) * 0.01
        return {'features': features, 'adj': adj, 'W': W, 'b': b}
    _L1_gnn_all = _L1_gnn_setup()
    _L1_gnn_in = {k: v for k, v in _L1_gnn_all.items() if k in ('W', 'b')}
    del _L1_gnn_all
    return {'x': x, 'adj': adj, 'L0_gnn_key': _L0_gnn_in['key'], 'L0_gnn_value': _L0_gnn_in['value'], 'L0_gnn_Wq': _L0_gnn_in['Wq'], 'L0_gnn_bq': _L0_gnn_in['bq'], 'L0_gnn_Wk': _L0_gnn_in['Wk'], 'L0_gnn_bk': _L0_gnn_in['bk'], 'L0_gnn_Wv': _L0_gnn_in['Wv'], 'L0_gnn_bv': _L0_gnn_in['bv'], 'L0_gnn_Wm': _L0_gnn_in['Wm'], 'L0_gnn_bm': _L0_gnn_in['bm'], 'L1_gnn_W': _L1_gnn_in['W'], 'L1_gnn_b': _L1_gnn_in['b']}

def reference(x, adj, L0_gnn_key, L0_gnn_value, L0_gnn_Wq, L0_gnn_bq, L0_gnn_Wk, L0_gnn_bk, L0_gnn_Wv, L0_gnn_bv, L0_gnn_Wm, L0_gnn_bm, L1_gnn_W, L1_gnn_b):
    import jax
    import jax.numpy as jnp

    def _L0_gnn_ref(query, key, value, adj_matrix, Wq, bq, Wk, bk, Wv, bv, Wm, bm):
        import jax, jax.numpy as jnp
        import numpy as np
        N = 4096
        D = 512
        q = query @ Wq.T + bq
        k = key @ Wk.T + bk
        v = value @ Wv.T + bv
        scale = q.shape[0] ** 0.5
        scores = jnp.einsum('nd,md->nm', q, k) / scale
        adj_scores = scores * adj_matrix
        adj_scores = jnp.where(jnp.abs(adj_scores) < 1e-05, -1000000000.0, adj_scores)
        prob = jax.nn.softmax(adj_scores, axis=-1)
        x = jnp.einsum('nm,md->nd', prob, v)
        return x @ Wm.T + bm

    def _L1_gnn_ref(features, adj, W, b):
        import jax, jax.numpy as jnp
        import numpy as np
        N = 4096
        D_IN = 512
        D_OUT = 512
        agg = adj @ features
        out = jnp.einsum('nd,od->no', agg, W) + b
        return jax.nn.relu(out)
    x = _layernorm(x + _L0_gnn_ref(x, L0_gnn_key, L0_gnn_value, adj, L0_gnn_Wq, L0_gnn_bq, L0_gnn_Wk, L0_gnn_bk, L0_gnn_Wv, L0_gnn_bv, L0_gnn_Wm, L0_gnn_bm), axis=-1)
    x = _layernorm(x + _L1_gnn_ref(x, adj, L1_gnn_W, L1_gnn_b), axis=-1)
    return x

_drawn_inputs = setup_inputs


def setup_inputs(seed=0):
    import zlib

    import numpy as np

    out = dict(_drawn_inputs(seed))
    spreads = {}
    factors = {'L0_gnn_bq': 59.846,
     'L0_gnn_bk': 64.0,
     'L0_gnn_bv': 4.564,
     'L0_gnn_bm': 4.379,
     'L1_gnn_b': 8.0}
    for name, (base, spread) in spreads.items():
        noise = np.random.default_rng([zlib.crc32(name.encode()), seed]).standard_normal(out[name].shape)
        drawn = base * np.exp(spread * noise) if base else spread * noise
        out[name] = jnp.asarray(drawn.astype(out[name].dtype))
    for name, factor in factors.items():
        out[name] = (out[name] * factor).astype(out[name].dtype)
    return out
```

```python
import concourse.bass as bass
from concourse import mybir
from contextlib import ExitStack

fp32 = mybir.dt.float32
f32r = mybir.dt.float32r
fp16 = mybir.dt.float16
bf16 = mybir.dt.bfloat16
ALU = mybir.AluOpType
ACT = mybir.ActivationFunctionType
AX = mybir.AxisListType

HI, LO = 0, 1
PASSES = ((HI, HI), (LO, HI), (HI, LO))


def wait(eng, sem, value):
    if not isinstance(value, int) or value > 0:
        eng.wait_ge(sem, value)


def attention_then_aggregation(nc, x, adj, key, value, wq, bq, wk, bk, wv, bv, wm, bm, w1, b1, out):
    N, D = x.shape
    P = 128
    KD = D // P
    NT = N // P
    HALF = N // 2
    MT = HALF // P
    C = 512
    MC = HALF // C
    TC = C // P
    SCALE = 1.0 / float(N) ** 0.5
    EPS_SCORE = 1e-5
    MASKED = -1e9
    EPS_LN = 1e-5

    ctx = ExitStack()

    def sb(scope, name, shape, dt):
        return scope.enter_context(nc.sbuf_tensor(name, shape, dt))

    def sem(name):
        return ctx.enter_context(nc.semaphore(name))

    t_dram = nc.dram_tensor("t_dram", [NT, P, 2 * D], fp32).ap()
    kt_dram = nc.dram_tensor("kt_dram", [P, 2, KD, HALF], fp32).ap()
    vp_dram = nc.dram_tensor("vp_dram", [P, 2, MT, D], fp32).ap()
    o_dram = nc.dram_tensor("o_dram", [N, D], fp32).ap()
    adj_bf = nc.dram_tensor("adj_bf", [N, N], bf16).ap()
    z_dram = nc.dram_tensor("z_dram", [N, D], fp32).ap()

    with ctx:
        ps = ctx.enter_context(nc.psum_tensor("ps", [P, 8, C], fp32))
        ident = sb(ctx, "ident", [P, P], fp32)
        c_all = sb(ctx, "c_all", [P, NT], fp32)
        bias_o = sb(ctx, "bias_o", [P, D], fp32)
        neg_max = sb(ctx, "neg_max", [P, NT, 2], fp32)
        row_sum = sb(ctx, "row_sum", [P, NT, 2], fp32)
        stats = sb(ctx, "stats", [P, NT, 2], fp32)

        resident = ctx.enter_context(ExitStack())
        KT = sb(resident, "KT", [P, 2, KD, HALF], f32r)
        VP = sb(resident, "VP", [P, 2, MT, D], f32r)
        prep = resident.enter_context(ExitStack())
        Aq = sb(prep, "Aq", [P, 2, KD, D], f32r)
        Wvm = sb(prep, "Wvm", [P, 2, KD, D], f32r)
        bq_k = sb(prep, "bq_k", [P, D], fp32)
        bk_q = sb(prep, "bk_q", [P, D], fp32)
        bqbk = sb(prep, "bqbk", [P, 1], fp32)

        raw = ExitStack()
        wa = sb(raw, "wa", [P, KD, D], fp32)
        wb = sb(raw, "wb", [P, KD, D], fp32)
        wc = sb(raw, "wc", [P, KD, D], fp32)
        wd = sb(raw, "wd", [P, KD, D], fp32)
        bcol = sb(raw, "bcol", [P, 3, KD], fp32)
        brep = sb(raw, "brep", [P, 3, KD, P], fp32)
        ones = sb(raw, "ones", [P, P], fp32)
        s_ident, s_one = sem("ident_made"), sem("ones_made")
        s_w = [sem("wq_wk_in%d" % e) for e in range(KD)]
        s_wv, s_wm, s_bc, s_bm = sem("wv_in"), sem("wm_in"), sem("bias_columns_in"), sem("bm_in")
        s_rep = sem("bias_repeated")
        s_amm, s_ahi, s_alo = sem("aq_made"), sem("aq_hi"), sem("aq_lo")
        s_rmm, s_rout = sem("bias_rows_made"), sem("bias_rows_out")
        s_wmt, s_wmc = sem("wm_transposed"), sem("wm_out")
        s_vmm, s_vhi, s_vlo = sem("wvm_made"), sem("wvm_hi"), sem("wvm_lo")
        s_bmm, s_bout = sem("bias_o_made"), sem("bias_o_out")
        with nc.Block() as block:

            @block.gpsimd
            def _(pool):
                nc.gpsimd.memset(ident[:, :], 0.0).then_inc(s_ident, 1)
                nc.gpsimd.memset(ones[:, :], 1.0).then_inc(s_one, 1)
                pool.wait_ge(s_ident, 1)
                nc.gpsimd.affine_select(out=ident[:, :], in_=ident[:, :], compare_op=ALU.not_equal, fill=1.0,
                                        base=0, pattern=[[-1, P]], channel_multiplier=1).then_inc(s_ident, 1)

            @block.sync
            def _(sp):
                for e in range(KD):
                    sp.dma_start(wa[:, e, :], wq[e * P:(e + 1) * P, :]).then_inc(s_w[e], 16)
                    sp.dma_start(wb[:, e, :], wk[e * P:(e + 1) * P, :]).then_inc(s_w[e], 16)
                with nc.allow_non_contiguous_dma(reason="three bias vectors, once"):
                    for n, b in enumerate((bq, bk, bv)):
                        sp.dma_start(bcol[:, n, :], b.rearrange("(k p) -> p k", p=P)).then_inc(s_bc, 16)
                sp.dma_start(bias_o[:, :], bm.rearrange("(a n) -> a n", a=1).to_broadcast([P, D])).then_inc(s_bm, 16)
                sp.dma_start(wc[:, :, :], wv.rearrange("(e p) d -> p e d", p=P)).then_inc(s_wv, 16)
                sp.dma_start(wd[:, :, :], wm.rearrange("(o p) e -> p o e", p=P)).then_inc(s_wm, 16)

            @block.tensor
            def _(pe):
                for e in range(KD):
                    pe.wait_ge(s_w[e], 32)
                    for d in range(KD):
                        last = nc.tensor.matmul(ps[:, d, :], wa[:, e, d * P:(d + 1) * P], wb[:, e, :],
                                                start=(e == 0), stop=(e == KD - 1))
                        if e == KD - 1:
                            last.then_inc(s_amm, 1)
                pe.wait_ge(s_rep, 3)
                for bank, b, w in ((4, 0, wb), (5, 1, wa)):
                    for e in range(KD):
                        last = nc.tensor.matmul(ps[:, bank, :], brep[:, b, e, :], w[:, e, :],
                                                start=(e == 0), stop=(e == KD - 1))
                    last.then_inc(s_rmm, 1)
                for e in range(KD):
                    last = nc.tensor.matmul(ps[:, 6, 0:1], brep[:, 0, e, :], bcol[:, 1, e:e + 1],
                                            start=(e == 0), stop=(e == KD - 1))
                last.then_inc(s_rmm, 1)
                pe.wait_ge(s_wm, 16)
                pe.wait_ge(s_wv, 16)
                pe.wait_ge(s_ident, 2)
                pe.wait_ge(s_alo, KD)
                for e in range(KD):
                    for o in range(KD):
                        last = nc.tensor.transpose(ps[:, e, o * P:(o + 1) * P], wd[:, o, e * P:(e + 1) * P], ident[:, :])
                    last.then_inc(s_wmt, 1)
                pe.wait_ge(s_wmc, KD)
                pe.wait_ge(s_rout, 3)
                for d in range(KD):
                    for e in range(KD):
                        last = nc.tensor.matmul(ps[:, 4 + d, :], wc[:, e, d * P:(d + 1) * P], wb[:, e, :],
                                                start=(e == 0), stop=(e == KD - 1))
                    last.then_inc(s_vmm, 1)
                for e in range(KD):
                    last = nc.tensor.matmul(ps[:, 0, :], brep[:, 2, e, :], wb[:, e, :],
                                            start=(e == 0), stop=(e == KD - 1))
                last.then_inc(s_bmm, 1)

            @block.scalar
            def _(act):
                act.wait_ge(s_bc, 48)
                act.wait_ge(s_one, 1)
                for b in range(3):
                    for e in range(KD):
                        last = nc.scalar.activation(brep[:, b, e, :], ones[:, :], ACT.Copy, scale=bcol[:, b, e:e + 1])
                    last.then_inc(s_rep, 1)
                for d in range(KD):
                    act.wait_ge(s_amm, d + 1)
                    nc.scalar.activation(Aq[:, HI, d, :], ps[:, d, :], ACT.Copy, scale=SCALE).then_inc(s_ahi, 1)
                act.wait_ge(s_rmm, 3)
                for e in range(KD):
                    act.wait_ge(s_wmt, e + 1)
                    nc.scalar.activation(wb[:, e, :], ps[:, e, :], ACT.Copy).then_inc(s_wmc, 1)
                for d in range(KD):
                    act.wait_ge(s_vmm, d + 1)
                    nc.scalar.activation(Wvm[:, HI, d, :], ps[:, 4 + d, :], ACT.Copy).then_inc(s_vhi, 1)

            @block.vector
            def _(dve):
                for d in range(KD):
                    dve.wait_ge(s_ahi, d + 1)
                    nc.vector.scalar_tensor_tensor(out=Aq[:, LO, d, :], in0=ps[:, d, :], scalar=SCALE,
                                                   in1=Aq[:, HI, d, :].bitcast(fp32), op0=ALU.mult,
                                                   op1=ALU.subtract).then_inc(s_alo, 1)
                dve.wait_ge(s_rmm, 3)
                nc.vector.tensor_scalar(bq_k[:, :], ps[:, 4, :], SCALE, None, ALU.mult).then_inc(s_rout, 1)
                nc.vector.tensor_scalar(bk_q[:, :], ps[:, 5, :], SCALE, None, ALU.mult).then_inc(s_rout, 1)
                nc.vector.tensor_scalar(bqbk[:, :], ps[:, 6, 0:1], SCALE, None, ALU.mult).then_inc(s_rout, 1)
                for d in range(KD):
                    dve.wait_ge(s_vhi, d + 1)
                    nc.vector.tensor_tensor(Wvm[:, LO, d, :], ps[:, 4 + d, :], Wvm[:, HI, d, :].bitcast(fp32),
                                            ALU.subtract).then_inc(s_vlo, 1)
                dve.wait_ge(s_bmm, 1)
                dve.wait_ge(s_bm, 16)
                nc.vector.tensor_tensor(bias_o[:, :], ps[:, 0, :], bias_o[:, :], ALU.add).then_inc(s_bout, 1)

        raw.close()

        work = ExitStack()
        rows_a = sb(work, "rows_a", [P, 2, D], fp32)
        rows_b = sb(work, "rows_b", [P, 2, D], fp32)
        srcT = sb(work, "srcT", [P, 2, 2, D], f32r)
        t_full = sb(work, "t_full", [P, 2, D], fp32)
        t_split = sb(work, "t_split", [P, 2, 2 * D], f32r)
        c_tmp = sb(work, "c_tmp", [P, 2], fp32)
        xu = sb(work, "xu", [P, D], fp32)
        a_in = [sem("a_in%d" % b) for b in range(2)]
        b_in = [sem("b_in%d" % b) for b in range(2)]
        k_tr, k_hi, k_lo = sem("k_tr"), sem("k_hi"), sem("k_lo")
        v_tr, vt_hi, vt_lo = sem("v_tr"), sem("vt_hi"), sem("vt_lo")
        v_mm, vp_hi, vp_lo = sem("v_mm"), sem("vp_hi"), sem("vp_lo")
        kt_st, vp_st = sem("kt_st"), sem("vp_st")
        x_tr, xt_hi, xt_lo = sem("x_tr"), sem("xt_hi"), sem("xt_lo")
        c_sum, c_out = sem("c_sum"), sem("c_out")
        t_mm, t_add, t_tr, t_hi, t_lo = [sem(n) for n in ("t_mm", "t_add", "t_tr", "t_hi", "t_lo")]
        t_st = [sem("t_st%d" % b) for b in range(2)]
        BA, BB, BC = 0, 2, 4

        def transposes(bank, source, slot):
            for k in range(KD):
                last = nc.tensor.transpose(ps[:, bank, k * P:(k + 1) * P], source[:, slot, k * P:(k + 1) * P], ident[:, :])
            return last

        def project(bank, slot, w):
            n = 0
            for s, m in PASSES:
                for k in range(KD):
                    last = nc.tensor.matmul(ps[:, bank, :], srcT[:, slot, s, k * P:(k + 1) * P], w[:, m, k, :],
                                            start=(n == 0), stop=(n == 3 * KD - 1))
                    n += 1
            return last

        with nc.Block() as block:

            @block.sync
            def _(sp):
                def kv_loads(i, section):
                    half = (1 - section) * HALF
                    for b in range(2):
                        g = section * MT + 2 * i + b
                        wait(sp, k_tr, g - 1)
                        sp.dma_start(rows_a[:, b, :], key[bass.ds(half + (2 * i + b) * P, P), :]).then_inc(a_in[b], 16)
                        wait(sp, v_tr, g - 1)
                        sp.dma_start(rows_b[:, b, :], value[bass.ds(half + (2 * i + b) * P, P), :]).then_inc(b_in[b], 16)

                def x_loads(i):
                    for b in range(2):
                        g = 2 * i + b
                        wait(sp, x_tr, g - 1)
                        wait(sp, c_sum, g - 1)
                        sp.dma_start(rows_a[:, b, :], x[bass.ds(g * P, P), :]).then_inc(a_in[b], 16)

                kv_loads(0, 0)
                with sp.Fori(1, MT // 2) as i:
                    kv_loads(i, 0)
                sp.wait_ge(k_tr, MT)
                x_loads(0)
                sp.wait_ge(vp_lo, MT)
                with sp.Fori(1, NT // 2) as i:
                    sp.dma_start(vp_dram[:, :, bass.ds(i - 1, 1), :],
                                 VP[:, :, bass.ds(i - 1, 1), :].bitcast(fp32)).then_inc(vp_st, 16)
                    x_loads(i)
                sp.dma_start(vp_dram[:, :, MT - 1, :], VP[:, :, MT - 1, :].bitcast(fp32)).then_inc(vp_st, 16)
                sp.wait_ge(x_tr, NT)
                sp.wait_ge(c_sum, NT)
                kv_loads(0, 1)
                with sp.Fori(1, MT // 2) as i:
                    kv_loads(i, 1)

            @block.tensor
            def _(pe):
                def kv_project(g, b):
                    pe.wait_ge(vt_lo, g + 1)
                    wait(pe, vp_lo, g - 1)
                    project(BC + b, b, Wvm).then_inc(v_mm, 1)

                def kv_step(i, section, first):
                    for b in range(2):
                        g = section * MT + 2 * i + b
                        pe.wait_ge(a_in[b], 16 * (section * (MT // 2 + NT // 2) + i + 1))
                        wait(pe, k_lo, g - 1)
                        transposes(BA + b, rows_a, b).then_inc(k_tr, 1)
                        pe.wait_ge(b_in[b], 16 * (section * MT // 2 + i + 1))
                        wait(pe, vt_lo, g - 1)
                        transposes(BB + b, rows_b, b).then_inc(v_tr, 1)
                        if not (first and b == 0):
                            kv_project(g - 1, 1 - b)

                def kv(section):
                    for i in range(2):
                        kv_step(i, section, i == 0)
                    with pe.Fori(2, MT // 2) as i:
                        kv_step(i, section, False)
                    kv_project((section + 1) * MT - 1, 1)

                def x_step(g, b, i):
                    if i is not None:
                        pe.wait_ge(a_in[b], 16 * (MT // 2 + i + 1))
                        wait(pe, xt_lo, g - 1)
                        transposes(BA + b, rows_a, b).then_inc(x_tr, 1)
                    if not isinstance(g, int) or 1 <= g <= NT:
                        pe.wait_ge(xt_lo, g)
                        wait(pe, t_add, g - 2)
                        project(BC + 1 - b, 1 - b, Aq).then_inc(t_mm, 1)
                    if not isinstance(g, int) or g >= 2:
                        pe.wait_ge(t_add, g - 1)
                        wait(pe, t_lo, g - 3)
                        transposes(BB + b, t_full, b).then_inc(t_tr, 1)

                pe.wait_ge(s_ident, 2)
                kv(0)
                pe.wait_ge(k_lo, MT)
                pe.wait_ge(vp_lo, MT)
                for i in range(2):
                    for b in range(2):
                        x_step(2 * i + b, b, i)
                with pe.Fori(2, NT // 2) as i:
                    for b in range(2):
                        x_step(2 * i + b, b, i)
                for b in range(2):
                    x_step(NT + b, b, None)
                pe.wait_ge(xt_lo, NT)
                pe.wait_ge(t_add, NT)
                pe.wait_ge(t_lo, NT)
                kv(1)

            @block.scalar
            def _(act):
                def kv_value_out(g, tile, b):
                    act.wait_ge(v_mm, g + 1)
                    nc.scalar.activation(VP[:, HI, tile, :], ps[:, BC + b, :], ACT.Copy).then_inc(vp_hi, 1)

                def kv_step(i, section, first):
                    for b in range(2):
                        tile = 2 * i + b
                        g = section * MT + tile
                        act.wait_ge(k_tr, g + 1)
                        nc.scalar.activation(KT[:, HI, :, bass.ts(tile, P)],
                                             ps[:, BA + b, :].rearrange("p (k n) -> p k n", n=P),
                                             ACT.Copy).then_inc(k_hi, 1)
                        act.wait_ge(v_tr, g + 1)
                        wait(act, v_mm, g - 1)
                        nc.scalar.activation(srcT[:, b, HI, :], ps[:, BB + b, :], ACT.Copy).then_inc(vt_hi, 1)
                        if not (first and b == 0):
                            kv_value_out(g - 1, tile - 1, 1 - b)

                def kv(section):
                    for i in range(2):
                        kv_step(i, section, i == 0)
                    with act.Fori(2, MT // 2) as i:
                        kv_step(i, section, False)
                    kv_value_out((section + 1) * MT - 1, MT - 1, 1)

                def x_step(g, b, inside):
                    if inside:
                        act.wait_ge(x_tr, g + 1)
                        wait(act, t_mm, g - 1)
                        nc.scalar.activation(srcT[:, b, HI, :], ps[:, BA + b, :], ACT.Copy).then_inc(xt_hi, 1)
                    if not isinstance(g, int) or g >= 2:
                        act.wait_ge(t_tr, g - 1)
                        return True
                    return False

                kv(0)
                act.wait_ge(v_mm, MT)
                for b in range(2):
                    x_step(b, b, True)
                for b in range(2):
                    x_step(2 + b, b, True)
                    nc.scalar.activation(t_split[:, b, 0:D], ps[:, BB + b, :], ACT.Copy).then_inc(t_hi, 1)
                with act.Fori(2, NT // 2) as i:
                    for b in range(2):
                        x_step(2 * i + b, b, True)
                        act.wait_ge(t_st[b], 16 * (i - 1))
                        nc.scalar.activation(t_split[:, b, 0:D], ps[:, BB + b, :], ACT.Copy).then_inc(t_hi, 1)
                for b in range(2):
                    x_step(NT + b, b, False)
                    act.wait_ge(t_st[b], 16 * (NT // 2 - 1))
                    nc.scalar.activation(t_split[:, b, 0:D], ps[:, BB + b, :], ACT.Copy).then_inc(t_hi, 1)
                act.wait_ge(kt_st, 16 * 2 * KD * MC)
                act.wait_ge(vp_st, 16 * MT)
                kv(1)

            @block.vector
            def _(dve):
                def kv_value_out(g, tile, b):
                    dve.wait_ge(vp_hi, g + 1)
                    nc.vector.tensor_tensor(VP[:, LO, tile, :], ps[:, BC + b, :], VP[:, HI, tile, :].bitcast(fp32),
                                            ALU.subtract).then_inc(vp_lo, 1)

                def kv_step(i, section, first):
                    for b in range(2):
                        tile = 2 * i + b
                        g = section * MT + tile
                        dve.wait_ge(k_hi, g + 1)
                        nc.vector.tensor_tensor(KT[:, LO, :, bass.ts(tile, P)],
                                                ps[:, BA + b, :].rearrange("p (k n) -> p k n", n=P),
                                                KT[:, HI, :, bass.ts(tile, P)].bitcast(fp32),
                                                ALU.subtract).then_inc(k_lo, 1)
                        dve.wait_ge(vt_hi, g + 1)
                        nc.vector.tensor_tensor(srcT[:, b, LO, :], ps[:, BB + b, :], srcT[:, b, HI, :].bitcast(fp32),
                                                ALU.subtract).then_inc(vt_lo, 1)
                        if not (first and b == 0):
                            kv_value_out(g - 1, tile - 1, 1 - b)

                def kv(section):
                    for i in range(2):
                        kv_step(i, section, i == 0)
                    with dve.Fori(2, MT // 2) as i:
                        kv_step(i, section, False)
                    kv_value_out((section + 1) * MT - 1, MT - 1, 1)

                def x_step(g, b, i):
                    if i is not None:
                        dve.wait_ge(xt_hi, g + 1)
                        nc.vector.tensor_tensor(srcT[:, b, LO, :], ps[:, BA + b, :], srcT[:, b, HI, :].bitcast(fp32),
                                                ALU.subtract).then_inc(xt_lo, 1)
                        wait(dve, c_out, g - 1)
                        nc.vector.tensor_tensor_reduce(out=xu[:, :], in0=rows_a[:, b, :], in1=bk_q[:, :], scale=1.0,
                                                       scalar=bqbk[:, 0:1], op0=ALU.mult, op1=ALU.add,
                                                       accum_out=c_tmp[:, b:b + 1]).then_inc(c_sum, 1)
                    if not isinstance(g, int) or 1 <= g <= NT:
                        dve.wait_ge(t_mm, g)
                        wait(dve, t_tr, g - 2)
                        nc.vector.tensor_tensor(t_full[:, 1 - b, :], ps[:, BC + 1 - b, :], bq_k[:, :],
                                                ALU.add).then_inc(t_add, 1)
                    if i is not None:
                        dve.wait_ge(c_sum, g + 1)
                        nc.vector.tensor_copy(c_all[:, bass.ds(g, 1)], c_tmp[:, b:b + 1]).then_inc(c_out, 1)
                    if not isinstance(g, int) or g >= 2:
                        dve.wait_ge(t_hi, g - 1)
                        nc.vector.tensor_tensor(t_split[:, b, D:2 * D], ps[:, BB + b, :],
                                                t_split[:, b, 0:D].bitcast(fp32), ALU.subtract).then_inc(t_lo, 1)

                kv(0)
                for i in range(2):
                    for b in range(2):
                        x_step(2 * i + b, b, i)
                with dve.Fori(2, NT // 2) as i:
                    for b in range(2):
                        x_step(2 * i + b, b, i)
                for b in range(2):
                    x_step(NT + b, b, None)
                kv(1)

            @block.gpsimd
            def _(pool):
                for c in range(MC):
                    pool.wait_ge(k_lo, TC * (c + 1))
                    for s in (HI, LO):
                        for k in range(KD):
                            pool.dma_start(kt_dram[:, s, k, c * C:(c + 1) * C],
                                           KT[:, s, k, c * C:(c + 1) * C].bitcast(fp32)).then_inc(kt_st, 16)
                with pool.Fori(0, NT // 2) as i:
                    for b in range(2):
                        pool.wait_ge(t_lo, 2 * i + b + 1)
                        pool.dma_start(t_dram[2 * i + b, :, :], t_split[:, b, :].bitcast(fp32)).then_inc(t_st[b], 16)
                for b in range(2):
                    pool.wait_ge(t_st[b], 16 * (NT // 2))

        work.close()
        prep.close()

        work = ExitStack()
        adj_rows = sb(work, "adj_rows", [P, 2, HALF], fp32)
        prob = sb(work, "prob", [P, 2, HALF], fp32)
        small = sb(work, "small", [P, 2, C], fp32)
        t_in = sb(work, "t_in", [P, 2, 2, D], f32r)
        probT = sb(work, "probT", [P, 2, 2, C], f32r)
        x_in = sb(work, "x_in", [P, 2, D], fp32)
        o_in = sb(work, "o_in", [P, 2, D], fp32)
        z_out = sb(work, "z_out", [P, 2, D], fp32)
        chunk_max = sb(work, "chunk_max", [P, 2, MC], fp32)
        nmax = sb(work, "nmax", [P, 2], fp32)
        rsum = sb(work, "rsum", [P, 2], fp32)
        nm_pair = sb(work, "nm_pair", [P, 2, 2], fp32)
        ls_pair = sb(work, "ls_pair", [P, 2, 2], fp32)
        nm = sb(work, "nm", [P, 2], fp32)
        wgt = sb(work, "wgt", [P, 2, 2], fp32)
        wls = sb(work, "wls", [P, 2, 2], fp32)
        den = sb(work, "den", [P, 2], fp32)
        rden = sb(work, "rden", [P, 2], fp32)
        wn = sb(work, "wn", [P, 2, 2], fp32)
        bst = sb(work, "bst", [P, 2, 6], fp32)
        mv = sb(work, "mv", [P, 2, 2], fp32)
        c_now = sb(work, "c_now", [P, 2], fp32)
        adj_in = [sem("adj_in%d" % b) for b in range(2)]
        q_in = [sem("q_in%d" % b) for b in range(2)]
        xo_in = [sem("xo_in%d" % b) for b in range(2)]
        kt_in = [sem("kt_in%d" % c) for c in range(MC)]
        vp_in = [sem("vp_in%d" % c) for c in range(MC)]
        s_mm, s_adj, s_abs, s_neg, s_mask = [sem(n) for n in ("s_mm", "s_adj", "s_abs", "s_neg", "s_mask")]
        s_max, s_exp, s_keep, s_c = sem("s_max"), sem("s_exp"), sem("s_keep"), sem("s_c")
        p_use, s_mv = sem("p_use"), sem("s_mv")
        p_tr, p_hi, p_lo, o_mm = [sem(n) for n in ("p_tr", "p_hi", "p_lo", "o_mm")]
        ab_st = [sem("ab_st%d" % b) for b in range(2)]
        o_out = sem("o_out")
        o_st = [sem("o_st%d" % b) for b in range(2)]
        m_step, m_w, xb = sem("m_step"), sem("m_w"), sem("xb")
        BS, BP, BO = 0, 4, 6

        with nc.Block() as block:

            @block.sync
            def _(sp):
                def loads(g, n, b, half):
                    wait(sp, s_mm, MC * (g - 1))
                    sp.dma_start(t_in[:, b, :, :].rearrange("p s d -> p (s d)").bitcast(fp32), t_dram[n, :, :])\
                      .then_inc(q_in[b], 16)
                    if not isinstance(g, int) or g >= 2:
                        sp.wait_ge(ab_st[b], 8 * (g - b))
                    sp.dma_start(adj_rows[:, b, :], adj[bass.ds(n * P, P), half * HALF:(half + 1) * HALF])\
                      .then_inc(adj_in[b], 16)

                def loads_x_o(n, b):
                    sp.dma_start(x_in[:, b, :], x[bass.ds(n * P, P), :]).then_inc(xo_in[b], 16)
                    sp.dma_start(o_in[:, b, :], o_dram[bass.ds(n * P, P), :]).then_inc(xo_in[b], 16)

                def store(g, n, b, half):
                    sp.wait_ge(o_out, g + 1)
                    dst = z_dram if half == 1 else o_dram
                    sp.dma_start(dst[bass.ds(n * P, P), :], z_out[:, b, :]).then_inc(o_st[b], 16)

                for n in range(3):
                    loads(n, n, n % 2, 0)
                with sp.Fori(1, NT // 2 - 1) as i:
                    for b in range(2):
                        loads(2 * i + b + 1, 2 * i + b + 1, 1 - b, 0)
                        store(2 * i + b - 2, 2 * i + b - 2, b, 0)
                loads(NT - 1, NT - 1, 1, 0)
                for n in (NT - 4, NT - 3):
                    store(n, n, n % 2, 0)
                for c in range(MC):
                    sp.wait_ge(s_mm, MC * (NT - 1) + c + 1)
                    sp.dma_start(KT[:, :, :, c * C:(c + 1) * C].rearrange("p s k n -> p (s k) n").bitcast(fp32),
                                 kt_dram[:, :, :, c * C:(c + 1) * C].rearrange("p s k n -> p (s k) n"))\
                      .then_inc(kt_in[c], 16)
                loads(NT, 0, 0, 1)
                store(NT - 2, NT - 2, 0, 0)
                loads(NT + 1, 1, 1, 1)
                sp.wait_ge(o_mm, NT)
                for c in range(MC):
                    if c == 2:
                        loads(NT + 2, 2, 0, 1)
                    sp.dma_start(VP[:, :, c * TC:(c + 1) * TC, :].bitcast(fp32),
                                 vp_dram[:, :, c * TC:(c + 1) * TC, :]).then_inc(vp_in[c], 16)
                store(NT - 1, NT - 1, 1, 0)
                for b in range(2):
                    sp.wait_ge(o_st[b], 16 * (NT // 2))
                for b in range(2):
                    loads_x_o(b, b)
                with sp.Fori(1, NT // 2 - 1) as i:
                    for b in range(2):
                        loads(NT + 2 * i + b + 1, 2 * i + b + 1, 1 - b, 1)
                        store(NT + 2 * i + b - 2, 2 * i + b - 2, b, 1)
                        loads_x_o(2 * i + b, b)
                loads(2 * NT - 1, NT - 1, 1, 1)
                for n in (NT - 4, NT - 3):
                    store(NT + n, n, n % 2, 1)
                    loads_x_o(n + 2, n % 2)
                for b in range(2):
                    store(2 * NT - 2 + b, NT - 2 + b, b, 1)
                for b in range(2):
                    sp.wait_ge(o_st[b], 16 * NT)

            @block.gpsimd
            def _(pool):
                for half in range(2):
                    with pool.Fori(0, NT // 2) as i:
                        for b in range(2):
                            pool.wait_ge(s_adj, MC * (half * NT + 2 * i + b + 1))
                            pool.dma_start(adj_bf[bass.ds((2 * i + b) * P, P), half * HALF:(half + 1) * HALF],
                                           adj_rows[:, b, :]).then_inc(ab_st[b], 16)
                for b in range(2):
                    pool.wait_ge(ab_st[b], 16 * NT)

            @block.tensor
            def _(pe):
                def scores(g, b, c):
                    wait(pe, s_adj, MC * (g - 1) + c + 1)
                    n = 0
                    for s, m in PASSES:
                        for k in range(KD):
                            last = nc.tensor.matmul(ps[:, BS + c, :], t_in[:, b, s, k * P:(k + 1) * P],
                                                    KT[:, m, k, c * C:(c + 1) * C],
                                                    start=(n == 0), stop=(n == 3 * KD - 1))
                            n += 1
                    last.then_inc(s_mm, 1)

                def turn(g, b, r):
                    if r == 0:
                        pe.wait_ge(s_exp, g + 1)
                    wait(pe, p_lo, MC * g + r - 1)
                    for j in range(TC):
                        m = r * TC + j
                        last = nc.tensor.transpose(ps[:, BP + r % 2, j * P:(j + 1) * P],
                                                   prob[:, b, m * P:(m + 1) * P], ident[:, :])
                    last.then_inc(p_tr, 1)

                def weigh(g, b, r):
                    if r == 0:
                        wait(pe, o_out, g - 1)
                    pe.wait_ge(p_lo, MC * g + r + 1)
                    for j in range(TC):
                        m = r * TC + j
                        for q, (s, v) in enumerate(PASSES):
                            last = nc.tensor.matmul(ps[:, BO + b, :], probT[:, r % 2, s, j * P:(j + 1) * P], VP[:, v, m, :],
                                                    start=(m == 0 and q == 0), stop=(m == MT - 1 and q == 2))
                    last.then_inc(o_mm, 1) if r == MC - 1 else last.then_inc(p_use, 1)

                def step(g, b, i, half, make, use):
                    if make:
                        pe.wait_ge(q_in[b], 16 * (half * NT // 2 + i + 1))
                    for c in range(MC):
                        if make:
                            if half == 1 and not use:
                                pe.wait_ge(kt_in[c], 16)
                            scores(g, b, c)
                        if use and c in (1, 2):
                            turn(g - 1, 1 - b, c - 1)
                    if use:
                        for r in range(MC):
                            if half == 1 and isinstance(i, int) and i == 0:
                                pe.wait_ge(vp_in[r], 16)
                            weigh(g - 1, 1 - b, r)
                            if r + 2 < MC:
                                turn(g - 1, 1 - b, r + 2)

                for half in range(2):
                    g0 = half * NT
                    step(g0, 0, 0, half, True, False)
                    step(g0 + 1, 1, 0, half, True, True)
                    for b in range(2):
                        step(g0 + 2 + b, b, 1, half, True, True)
                    with pe.Fori(2, NT // 2) as i:
                        for b in range(2):
                            step(g0 + 2 * i + b, b, i, half, True, True)
                    step(g0 + NT, 0, None, half, False, True)

            @block.scalar
            def _(act):
                def magnitude(g, b, c):
                    act.wait_ge(s_adj, MC * g + c + 1)
                    wait(act, s_mask, MC * g + c - 1)
                    nc.scalar.activation(small[:, c % 2, :], prob[:, b, c * C:(c + 1) * C], ACT.Abs).then_inc(s_abs, 1)

                def exponentials(g, b):
                    act.wait_ge(s_max, g + 1)
                    wait(act, s_keep, g - 1)
                    nc.scalar.activation(prob[:, b, :], prob[:, b, :], ACT.Exp, bias=nmax[:, b:b + 1],
                                         accum_out=rsum[:, b:b + 1]).then_inc(s_exp, 1)

                def turned(g, r):
                    act.wait_ge(p_tr, MC * g + r + 1)
                    slot_free(g, r)
                    nc.scalar.activation(probT[:, r % 2, HI, :], ps[:, BP + r % 2, :], ACT.Copy).then_inc(p_hi, 1)

                def slot_free(g, r):
                    if r >= 2:
                        act.wait_ge(p_use, (MC - 1) * g + r - 1)
                    elif r == 1:
                        wait(act, o_mm, g)
                    else:
                        wait(act, p_use, (MC - 1) * g)

                def step(g, b, half, make, use, merge):
                    for c in range(MC):
                        if make:
                            magnitude(g, b, c)
                        if use and c in (1, 2):
                            turned(g - 1, c - 1)
                        if merge and c == 1:
                            finish(g - 2, b, half)
                    if use:
                        turned(g - 1, 2)
                        turned(g - 1, 3)
                    if make:
                        exponentials(g, b)

                def finish(g, b, half):
                    if half == 0:
                        act.wait_ge(o_mm, g + 1)
                        if not isinstance(g, int) or g >= 2:
                            act.wait_ge(o_st[b], 8 * (g - b))
                        nc.scalar.activation(z_out[:, b, :], ps[:, BO + b, :], ACT.Copy).then_inc(o_out, 1)
                    else:
                        act.wait_ge(m_w, 2 * (g - NT) + 1)
                        nc.scalar.activation(wgt[:, b, :], nm_pair[:, b, :], ACT.Exp, bias=nm[:, b:b + 1],
                                             scale=-1.0).then_inc(m_w, 1)

                for half in range(2):
                    g0 = half * NT
                    step(g0, 0, half, True, False, False)
                    step(g0 + 1, 1, half, True, True, False)
                    for b in range(2):
                        step(g0 + 2 + b, b, half, True, True, True)
                    with act.Fori(2, NT // 2) as i:
                        for b in range(2):
                            step(g0 + 2 * i + b, b, half, True, True, True)
                    step(g0 + NT, 0, half, False, True, True)
                    finish(g0 + NT - 1, 1, half)

            @block.vector
            def _(dve):
                def masked(g, b, c, i, half):
                    if c == 0:
                        dve.wait_ge(adj_in[b], 16 * (half * NT // 2 + i + 1))
                        wait(dve, p_tr, MC * (g - 1))
                        nc.vector.tensor_copy(c_now[:, b:b + 1], c_all[:, bass.ds(2 * i + b, 1)]).then_inc(s_c, 1)
                        dve.wait_ge(s_c, g + 1)
                    dve.wait_ge(s_mm, MC * g + c + 1)
                    nc.vector.scalar_tensor_tensor(out=prob[:, b, c * C:(c + 1) * C], in0=ps[:, BS + c, :],
                                                   scalar=c_now[:, b:b + 1], in1=adj_rows[:, b, c * C:(c + 1) * C],
                                                   op0=ALU.add, op1=ALU.mult).then_inc(s_adj, 1)

                def small_scores(g, b, c):
                    dve.wait_ge(s_abs, MC * g + c + 1)
                    nc.vector.tensor_scalar(small[:, c % 2, :], small[:, c % 2, :], EPS_SCORE, MASKED,
                                            ALU.is_lt, ALU.mult).then_inc(s_neg, 1)

                def small_ready(g, c):
                    dve.wait_ge(s_neg, MC * g + c + 1)

                def threshold(b, c):
                    nc.vector.tensor_tensor_reduce(out=prob[:, b, c * C:(c + 1) * C], in0=prob[:, b, c * C:(c + 1) * C],
                                                   in1=small[:, c % 2, :], scale=1.0, scalar=-3.4e38, op0=ALU.add,
                                                   op1=ALU.max, accum_out=chunk_max[:, b, c:c + 1]).then_inc(s_mask, 1)

                def maximum(g, b, n, half):
                    dve.wait_ge(s_mask, MC * (g + 1))
                    wait(dve, s_exp, g - 1)
                    nc.vector.tensor_reduce(nmax[:, b:b + 1], chunk_max[:, b, :], AX.X, ALU.max, negate=True)\
                             .then_inc(s_max, 1)

                def keep_maximum(g, b, n, half):
                    dve.wait_ge(s_max, g + 1)
                    nc.vector.tensor_copy(neg_max[:, bass.ds(n, 1), half], nmax[:, b:b + 1])

                def keep_sum(g, b, n, half):
                    dve.wait_ge(s_exp, g + 1)
                    nc.vector.tensor_copy(row_sum[:, bass.ds(n, 1), half], rsum[:, b:b + 1]).then_inc(s_keep, 1)

                def turned(g, r):
                    dve.wait_ge(p_hi, MC * g + r + 1)
                    nc.vector.tensor_tensor(probT[:, r % 2, LO, :], ps[:, BP + r % 2, :],
                                            probT[:, r % 2, HI, :].bitcast(fp32), ALU.subtract).then_inc(p_lo, 1)

                def pick(g, b, n):
                    k = g - NT
                    nc.vector.tensor_copy(nm_pair[:, b, :], neg_max[:, bass.ds(n, 1), :].rearrange("p a h -> p (a h)"))
                    nc.vector.tensor_copy(ls_pair[:, b, :], row_sum[:, bass.ds(n, 1), :].rearrange("p a h -> p (a h)"))\
                             .then_inc(m_step, 1)
                    dve.wait_ge(m_step, 7 * k + 1)
                    nc.vector.tensor_reduce(nm[:, b:b + 1], nm_pair[:, b, :], AX.X, ALU.min).then_inc(m_w, 1)

                def merge(g, b, i):
                    k = g - NT
                    dve.wait_ge(m_w, 2 * k + 2)
                    nc.vector.tensor_tensor(wls[:, b, :], wgt[:, b, :], ls_pair[:, b, :], ALU.mult).then_inc(m_step, 1)
                    dve.wait_ge(m_step, 7 * k + 2)
                    nc.vector.reduce_sum(den[:, b:b + 1], wls[:, b, :], AX.X).then_inc(m_step, 1)
                    dve.wait_ge(m_step, 7 * k + 3)
                    nc.vector.reciprocal(rden[:, b:b + 1], den[:, b:b + 1]).then_inc(m_step, 1)
                    dve.wait_ge(m_step, 7 * k + 4)
                    nc.vector.tensor_scalar(wn[:, b, :], wgt[:, b, :], rden[:, b:b + 1], None, ALU.mult).then_inc(m_step, 1)
                    dve.wait_ge(xo_in[b], 32 * (i + 1))
                    dve.wait_ge(o_st[b], 16 * (NT // 2 + i))
                    nc.vector.tensor_tensor(x_in[:, b, :], x_in[:, b, :], bias_o[:, :], ALU.add).then_inc(xb, 1)
                    dve.wait_ge(m_step, 7 * k + 5)
                    dve.wait_ge(xb, k + 1)
                    nc.vector.scalar_tensor_tensor(out=x_in[:, b, :], in0=o_in[:, b, :], scalar=wn[:, b, 0:1],
                                                   in1=x_in[:, b, :], op0=ALU.mult, op1=ALU.add).then_inc(m_step, 1)
                    dve.wait_ge(o_mm, g + 1)
                    dve.wait_ge(m_step, 7 * k + 6)
                    nc.vector.scalar_tensor_tensor(out=z_out[:, b, :], in0=ps[:, BO + b, :], scalar=wn[:, b, 1:2],
                                                   in1=x_in[:, b, :], op0=ALU.mult, op1=ALU.add).then_inc(o_out, 1)
                    dve.wait_ge(o_out, g + 1)
                    nc.vector.bn_stats(bst[:, b, :], z_out[:, b, :]).then_inc(m_step, 1)

                def row_stats(g, b, n):
                    k = g - NT
                    nc.vector.bn_aggr(mv[:, b, :], bst[:, b, :]).then_inc(s_mv, 1)
                    dve.wait_ge(s_mv, k + 1)
                    nc.vector.tensor_copy(stats[:, bass.ds(n, 1), :].rearrange("p a h -> p (a h)"), mv[:, b, :])

                def step(g, b, i, half, make, use, fin):
                    n = None if i is None else 2 * i + b
                    fin = fin and half == 1
                    if use:
                        keep_sum(g - 1, 1 - b, (NT if n is None else n) - 1, half)
                    if fin:
                        pick(g - 2, b, (NT if n is None else n) - 2)
                    if make:
                        masked(g, b, 0, i, half)
                        masked(g, b, 1, i, half)
                        small_scores(g, b, 0)
                        small_ready(g, 0)
                    if use:
                        turned(g - 1, 0)
                    if make:
                        threshold(b, 0)
                    if make:
                        masked(g, b, 2, i, half)
                        small_scores(g, b, 1)
                        small_ready(g, 1)
                    if use:
                        turned(g - 1, 1)
                    if make:
                        threshold(b, 1)
                        masked(g, b, 3, i, half)
                        small_scores(g, b, 2)
                        small_ready(g, 2)
                        small_scores(g, b, 3)
                        threshold(b, 2)
                        small_ready(g, 3)
                    if use:
                        turned(g - 1, 2)
                    if make:
                        threshold(b, 3)
                        maximum(g, b, n, half)
                    if use:
                        turned(g - 1, 3)
                    if fin:
                        merge(g - 2, b, (NT // 2 if i is None else i) - 1)
                        dve.wait_ge(m_step, 7 * (g - 2 - NT) + 7)
                    if make:
                        keep_maximum(g, b, n, half)
                    if fin:
                        row_stats(g - 2, b, (NT if n is None else n) - 2)

                for half in range(2):
                    g0 = half * NT
                    step(g0, 0, 0, half, True, False, False)
                    step(g0 + 1, 1, 0, half, True, True, False)
                    for b in range(2):
                        step(g0 + 2 + b, b, 1, half, True, True, True)
                    with dve.Fori(2, NT // 2) as i:
                        for b in range(2):
                            step(g0 + 2 * i + b, b, i, half, True, True, True)
                    step(g0 + NT, 0, None, half, False, True, True)
                    if half == 1:
                        pick(g0 + NT - 1, 1, NT - 1)
                        merge(g0 + NT - 1, 1, NT // 2 - 1)
                        dve.wait_ge(m_step, 7 * NT)
                        row_stats(g0 + NT - 1, 1, NT - 1)

        work.close()
        resident.close()

        work = ExitStack()
        WT = sb(work, "WT", [P, 2, KD, D], f32r)
        X1 = sb(work, "X1", [P, 2, NT, D], fp16)
        b1_rep = sb(work, "b1_rep", [P, D], fp32)
        w_raw = sb(work, "w_raw", [P, KD, D], fp32)
        z_in = sb(work, "z_in", [P, 2, TC, D], fp32)
        std = sb(work, "std", [P, NT, 1], fp32)
        rstd = sb(work, "rstd", [P, NT, 1], fp32)
        QUARTER = N // 4
        QT = QUARTER // P
        adjT = sb(work, "adjT", [P, 4, QT, C], bf16)
        G = sb(work, "G", [P, 2, KD, C], f32r)
        zf = sb(work, "zf", [P, 2, D], fp32)
        y = sb(work, "y", [P, 2, D], fp32)
        res = sb(work, "res", [P, 2, D], fp32)
        bst2 = sb(work, "bst2", [P, 2, 6], fp32)
        mv2 = sb(work, "mv2", [P, 2, 2], fp32)
        vare = sb(work, "vare", [P, 2], fp32)
        std2 = sb(work, "std2", [P, 2], fp32)
        rstd2 = sb(work, "rstd2", [P, 2], fp32)
        st_now = sb(work, "st_now", [P, 2, 3], fp32)
        w_in, b1_in, n_var, n_std, n_rstd = [sem(n) for n in ("w_in", "b1_in", "n_var", "n_std", "n_rstd")]
        zg_in = [sem("zg_in%d" % b) for b in range(2)]
        x1_full, x1_hi, x1_lo = sem("x1_full"), sem("x1_hi"), sem("x1_lo")
        w_tr, w_hi, w_lo = sem("w_tr"), sem("w_hi"), sem("w_lo")
        aq_in = [sem("aq_in%d" % q) for q in range(4)]
        a_use = sem("a_use")
        g_mm, g_hi, g_lo = sem("g_mm"), sem("g_hi"), sem("g_lo")
        f_mm, f_out = sem("f_mm"), sem("f_out")
        zf_in = [sem("zf_in%d" % b) for b in range(2)]
        f_x1, f_sum, f_bn = sem("f_x1"), sem("f_sum"), sem("f_bn")
        f_var, f_std, f_res = sem("f_var"), sem("f_std"), sem("f_res")
        f_mv, f_rstd = sem("f_mv"), sem("f_rstd")
        out_st = [sem("out_st%d" % b) for b in range(2)]
        BG, BF = 0, 6
        NB = N // C
        FIRST_F, NEXT_F = 2, 3

        with nc.Block() as block:

            @block.sync
            def _(sp):
                def z_group(i, b):
                    wait(sp, x1_lo, TC * (2 * i + b - 1))
                    sp.dma_start(z_in[:, b, :, :],
                                 z_dram[bass.ds((2 * i + b) * C, C), :].rearrange("(k p) d -> p k d", p=P))\
                      .then_inc(zg_in[b], 16)

                def adj_quarter(nb, q):
                    sp.dma_start_transpose(adjT[:, q, :, :], adj_bf[bass.ds(nb * C, C), q * QUARTER:(q + 1) * QUARTER])\
                      .then_inc(aq_in[q], 16)

                for i in range(NB // 2):
                    for b in range(2):
                        z_group(i, b)
                        if b == 0:
                            adj_quarter(0, i)
                    if i == 0:
                        sp.dma_start(w_raw[:, :, :], w1.rearrange("(o p) e -> p o e", p=P)).then_inc(w_in, 16)
                        sp.dma_start(b1_rep[:, :], b1.rearrange("(a n) -> a n", a=1).to_broadcast([P, D])).then_inc(b1_in, 16)
                with sp.Fori(1, NB) as nb:
                    for q in range(4):
                        if q < 3:
                            sp.wait_ge(a_use, 3 * (nb - 1) + q + 1)
                        else:
                            sp.wait_ge(g_mm, KD * nb)
                        adj_quarter(nb, q)

            @block.tensor
            def _(pe):
                def second_weights():
                    pe.wait_ge(w_in, 16)
                    for e in range(KD):
                        for o in range(KD):
                            last = nc.tensor.transpose(ps[:, 4 + e, o * P:(o + 1) * P], w_raw[:, o, e * P:(e + 1) * P],
                                                       ident[:, :])
                        last.then_inc(w_tr, 1)

                def aggregate(nb, m):
                    q = m // QT
                    if m % QT == 0:
                        pe.wait_ge(aq_in[q], 16 * (nb + 1))
                    for d in range(KD):
                        if m == 0:
                            wait(pe, g_lo, KD * (nb - 1) + d + 1)
                        for s in (HI, LO):
                            last = nc.tensor.matmul(ps[:, BG + d, :], X1[:, s, m, d * P:(d + 1) * P], adjT[:, q, m % QT, :],
                                                    start=(m == 0 and s == HI), stop=(m == NT - 1 and s == LO))
                        if m == NT - 1:
                            last.then_inc(g_mm, 1)
                    if m % QT == QT - 1 and m < NT - 1:
                        last.then_inc(a_use, 1)

                def output(nb, k):
                    pe.wait_ge(g_lo, KD * (nb + 1))
                    wait(pe, f_out, TC * nb + max(k - 1, 0))
                    n = 0
                    for s, w in PASSES:
                        for d in range(KD):
                            last = nc.tensor.matmul(ps[:, BF + k % 2, :], G[:, s, d, k * P:(k + 1) * P], WT[:, w, d, :],
                                                    start=(n == 0), stop=(n == 3 * KD - 1))
                            n += 1
                    last.then_inc(f_mm, 1)

                def rows(nb, outputs):
                    for m in range(NT):
                        if outputs is None:
                            pe.wait_ge(x1_lo, m + 1)
                            if m == QT:
                                second_weights()
                        aggregate(nb, m)
                        if outputs is not None and m >= FIRST_F and (m - FIRST_F) % NEXT_F == 0 \
                                and (m - FIRST_F) // NEXT_F < TC:
                            output(outputs, (m - FIRST_F) // NEXT_F)

                rows(0, None)
                pe.wait_ge(w_lo, KD)
                rows(1, 0)
                with pe.Fori(2, NB) as nb:
                    rows(nb, nb - 1)
                for k in range(TC):
                    output(NB - 1, k)

            @block.scalar
            def _(act):
                act.wait_ge(n_var, 1)
                nc.scalar.activation(std[:, :, :], std[:, :, :], ACT.Sqrt).then_inc(n_std, 1)
                def x1_tiles(i):
                    for b in range(2):
                        for k in range(TC):
                            n = TC * (2 * i + b) + k
                            act.wait_ge(x1_full, n + 1)
                            nc.scalar.activation(X1[:, HI, bass.ds(n, 1), :].rearrange("p a d -> p (a d)"),
                                                 z_in[:, b, k, :], ACT.Copy).then_inc(x1_hi, 1)

                with act.Fori(0, NB // 2) as i:
                    x1_tiles(i)
                for e in range(KD):
                    act.wait_ge(w_tr, e + 1)
                    nc.scalar.activation(WT[:, HI, e, :], ps[:, 4 + e, :], ACT.Copy).then_inc(w_hi, 1)

                def root(nb, k):
                    act.wait_ge(f_var, TC * nb + k + 1)
                    nc.scalar.activation(std2[:, k % 2:k % 2 + 1], vare[:, k % 2:k % 2 + 1], ACT.Sqrt).then_inc(f_std, 1)

                def rows(nb, outputs):
                    if outputs is not None:
                        for k in range(TC):
                            root(outputs, k)
                        act.wait_ge(f_mm, TC * (outputs + 1))
                    for d in range(KD):
                        act.wait_ge(g_mm, KD * nb + d + 1)
                        nc.scalar.activation(G[:, HI, d, :], ps[:, BG + d, :], ACT.Copy).then_inc(g_hi, 1)

                rows(0, None)
                with act.Fori(1, NB) as nb:
                    rows(nb, nb - 1)
                for k in range(TC):
                    root(NB - 1, k)

            @block.vector
            def _(dve):
                nc.vector.tensor_scalar(std[:, :, :], stats[:, :, 1:2], EPS_LN, None, ALU.add).then_inc(n_var, 1)
                dve.wait_ge(n_std, 1)
                nc.vector.reciprocal(rstd[:, :, :], std[:, :, :]).then_inc(n_rstd, 1)
                dve.wait_ge(n_rstd, 1)
                with dve.Fori(0, NB // 2) as i:
                    for b in range(2):
                        dve.wait_ge(zg_in[b], 16 * (i + 1))
                        for k in range(TC):
                            n = TC * (2 * i + b) + k
                            nc.vector.tensor_scalar(z_in[:, b, k, :], z_in[:, b, k, :], stats[:, bass.ds(n, 1), 0],
                                                    rstd[:, bass.ds(n, 1), 0], ALU.subtract, ALU.mult)\
                                     .then_inc(x1_full, 1)
                        for k in range(TC):
                            n = TC * (2 * i + b) + k
                            dve.wait_ge(x1_hi, n + 1)
                            nc.vector.tensor_tensor(X1[:, LO, bass.ds(n, 1), :].rearrange("p a d -> p (a d)"),
                                                    z_in[:, b, k, :],
                                                    X1[:, HI, bass.ds(n, 1), :].rearrange("p a d -> p (a d)"),
                                                    ALU.subtract).then_inc(x1_lo, 1)

                for e in range(KD):
                    dve.wait_ge(w_hi, e + 1)
                    nc.vector.tensor_tensor(WT[:, LO, e, :], ps[:, 4 + e, :], WT[:, HI, e, :].bitcast(fp32),
                                            ALU.subtract).then_inc(w_lo, 1)

                def normalised(nb, k):
                    t = TC * nb + k
                    b = k % 2
                    dve.wait_ge(zf_in[b], 16 * (2 * nb + k // 2 + 1))
                    nc.vector.tensor_scalar(zf[:, b, :], zf[:, b, :], stats[:, bass.ds(t, 1), 0],
                                            rstd[:, bass.ds(t, 1), 0], ALU.subtract, ALU.mult).then_inc(f_x1, 1)

                def second_layer(nb, k):
                    t = TC * nb + k
                    b = k % 2
                    dve.wait_ge(f_mm, t + 1)
                    nc.vector.tensor_tensor(y[:, b, :], ps[:, BF + b, :], b1_rep[:, :], ALU.add).then_inc(f_out, 1)
                    dve.wait_ge(f_x1, t + 1)
                    dve.wait_ge(f_out, t + 1)
                    nc.vector.scalar_tensor_tensor(out=y[:, b, :], in0=y[:, b, :], scalar=0.0, in1=zf[:, b, :],
                                                   op0=ALU.max, op1=ALU.add).then_inc(f_sum, 1)
                    dve.wait_ge(f_sum, t + 1)
                    nc.vector.bn_stats(bst2[:, b, :], y[:, b, :]).then_inc(f_bn, 1)
                    dve.wait_ge(f_bn, t + 1)

                def variance(nb, k):
                    t = TC * nb + k
                    b = k % 2
                    nc.vector.bn_aggr(mv2[:, b, :], bst2[:, b, :]).then_inc(f_mv, 1)
                    dve.wait_ge(f_mv, t + 1)
                    nc.vector.tensor_scalar(vare[:, b:b + 1], mv2[:, b, 1:2], EPS_LN, None, ALU.add).then_inc(f_var, 1)

                def result(nb, k):
                    t = TC * nb + k
                    b = k % 2
                    dve.wait_ge(f_std, t + 1)
                    nc.vector.reciprocal(rstd2[:, b:b + 1], std2[:, b:b + 1]).then_inc(f_rstd, 1)
                    dve.wait_ge(f_rstd, t + 1)
                    wait(dve, out_st[b], 16 * (2 * nb + k // 2))
                    nc.vector.tensor_scalar(res[:, b, :], y[:, b, :], mv2[:, b, 0:1], rstd2[:, b:b + 1],
                                            ALU.subtract, ALU.mult).then_inc(f_res, 1)

                def outputs(nb):
                    normalised(nb, 0)
                    second_layer(nb, 0)
                    normalised(nb, 1)
                    variance(nb, 0)
                    for k in range(1, TC):
                        second_layer(nb, k)
                        result(nb, k - 1)
                        variance(nb, k)
                        if k + 1 < TC:
                            normalised(nb, k + 1)
                    result(nb, TC - 1)

                def g_split(nb):
                    for d in range(KD):
                        dve.wait_ge(g_hi, KD * nb + d + 1)
                        nc.vector.tensor_tensor(G[:, LO, d, :], ps[:, BG + d, :], G[:, HI, d, :].bitcast(fp32),
                                                ALU.subtract).then_inc(g_lo, 1)

                dve.wait_ge(b1_in, 16)
                g_split(0)
                outputs(0)
                g_split(1)
                with dve.Fori(2, NB) as nb:
                    outputs(nb - 1)
                    g_split(nb)
                outputs(NB - 1)

            @block.gpsimd
            def _(pool):
                def z_load(t, b):
                    pool.dma_start(zf[:, b, :], z_dram[bass.ds(t * P, P), :]).then_inc(zf_in[b], 16)

                def store(t, b):
                    pool.wait_ge(f_res, t + 1)
                    pool.dma_start(out[bass.ds(t * P, P), :], res[:, b, :]).then_inc(out_st[b], 16)

                for b in range(2):
                    z_load(b, b)
                with pool.Fori(0, NT // 2 - 1) as i:
                    for b in range(2):
                        store(2 * i + b, b)
                        z_load(2 * i + 2 + b, b)
                for b in range(2):
                    store(NT - 2 + b, b)
                for b in range(2):
                    pool.wait_ge(out_st[b], 16 * (NT // 2))

        work.close()


_INS = ["x", "adj", "L0_gnn_key", "L0_gnn_value", "L0_gnn_Wq", "L0_gnn_bq", "L0_gnn_Wk", "L0_gnn_bk", "L0_gnn_Wv",
        "L0_gnn_bv", "L0_gnn_Wm", "L0_gnn_bm", "L1_gnn_W", "L1_gnn_b"]


def kernel(**inputs):
    import numpy as _np
    import concourse.bacc as _bacc
    from concourse.bass_utils import run_bass_kernel_spmd as _run

    nc = _bacc.Bacc("TRN2", target_bir_lowering=False, num_devices=1)
    arrays, args = {}, []
    for name in _INS:
        a = _np.ascontiguousarray(inputs[name])
        arrays["in_" + name] = a
        args.append(nc.dram_tensor("in_" + name, a.shape, mybir.dt.from_np(a.dtype), kind="ExternalInput").ap())
    args.append(nc.dram_tensor("out_0", (4096, 512), fp32, kind="ExternalOutput").ap())
    attention_then_aggregation(nc, *args)
    r = _run(nc, [arrays], core_ids=[0])
    return r.results[0]["out_0"]
```

```python
import concourse.bass as bass
from concourse import mybir
from contextlib import ExitStack

fp32 = mybir.dt.float32
f32r = mybir.dt.float32r
fp16 = mybir.dt.float16
bf16 = mybir.dt.bfloat16
ALU = mybir.AluOpType
ACT = mybir.ActivationFunctionType
AX = mybir.AxisListType

HI, LO = 0, 1
PASSES = ((HI, HI), (LO, HI), (HI, LO))


def wait(eng, sem, value):
    if not isinstance(value, int) or value > 0:
        eng.wait_ge(sem, value)


def attention_then_aggregation(nc, x, adj, key, value, wq, bq, wk, bk, wv, bv, wm, bm, w1, b1, out):
    N, D = x.shape
    P = 128
    KD = D // P
    NT = N // P
    HALF = N // 2
    MT = HALF // P
    C = 512
    MC = HALF // C
    TC = C // P
    SCALE = 1.0 / float(N) ** 0.5
    EPS_SCORE = 1e-5
    MASKED = -1e9
    EPS_LN = 1e-5

    ctx = ExitStack()

    def sb(scope, name, shape, dt):
        return scope.enter_context(nc.sbuf_tensor(name, shape, dt))

    def sem(name):
        return ctx.enter_context(nc.semaphore(name))

    t_dram = nc.dram_tensor("t_dram", [NT, P, 2 * D], fp32).ap()
    kt_dram = nc.dram_tensor("kt_dram", [P, 2, KD, HALF], fp32).ap()
    vp_dram = nc.dram_tensor("vp_dram", [P, 2, MT, D], fp32).ap()
    o_dram = nc.dram_tensor("o_dram", [N, D], fp32).ap()
    adj_bf = nc.dram_tensor("adj_bf", [N, N], bf16).ap()
    z_dram = nc.dram_tensor("z_dram", [N, D], fp32).ap()

    with ctx:
        ps = ctx.enter_context(nc.psum_tensor("ps", [P, 8, C], fp32))
        ident = sb(ctx, "ident", [P, P], fp32)
        c_all = sb(ctx, "c_all", [P, NT], fp32)
        bias_o = sb(ctx, "bias_o", [P, D], fp32)
        neg_max = sb(ctx, "neg_max", [P, NT, 2], fp32)
        row_sum = sb(ctx, "row_sum", [P, NT, 2], fp32)
        stats = sb(ctx, "stats", [P, NT, 2], fp32)

        resident = ctx.enter_context(ExitStack())
        KT = sb(resident, "KT", [P, 2, KD, HALF], f32r)
        with ExitStack() as raw:
            wa = sb(raw, "wa", [P, KD, D], fp32)
            wb = sb(raw, "wb", [P, KD, D], fp32)
            wd = sb(raw, "wd", [P, KD, D], fp32)
            wc = sb(raw, "wc", [P, KD, D], fp32)
        VP = sb(resident, "VP", [P, 2, MT, D], f32r)
        prep = resident.enter_context(ExitStack())
        Aq = sb(prep, "Aq", [P, 2, KD, D], f32r)
        Wvm = sb(prep, "Wvm", [P, 2, KD, D], f32r)
        bq_k = sb(prep, "bq_k", [P, KD], fp32)
        bk_q = sb(prep, "bk_q", [P, D], fp32)
        bqbk = sb(prep, "bqbk", [P, 1], fp32)

        wmT = sb(prep, "wmT", [P, KD, D], fp32)
        bcol = sb(prep, "bcol", [P, 3, KD], fp32)
        brep = sb(prep, "brep", [P, 3, KD, P], fp32)
        ones = sb(prep, "ones", [P, P], fp32)
        s_ident, s_one = sem("ident_made"), sem("ones_made")
        s_w = [sem("wq_wk_in%d" % e) for e in range(KD)]
        s_wv, s_wm, s_bc, s_bm = sem("wv_in"), sem("wm_in"), sem("bias_columns_in"), sem("bm_in")
        s_rep = sem("bias_repeated")
        s_amm, s_ahi, s_alo = sem("aq_made"), sem("aq_hi"), sem("aq_lo")
        s_rmm, s_rout = sem("bias_rows_made"), sem("bias_rows_out")
        s_wmt, s_wmc = sem("wm_transposed"), sem("wm_out")
        s_vmm, s_vhi, s_vlo = sem("wvm_made"), sem("wvm_hi"), sem("wvm_lo")
        s_bmm, s_bout = sem("bias_o_made"), sem("bias_o_out")

        work = ExitStack()
        rows = sb(work, "rows", [P, 4, D], fp32)
        valueT = sb(work, "valueT", [P, 2, 2, D], f32r)
        c_tmp = sb(work, "c_tmp", [P, 2], fp32)
        xu = sb(work, "xu", [P, D], fp32)
        row_in = [sem("row_in%d" % j) for j in range(4)]
        x_tr, xt_hi, xt_lo = sem("x_tr"), sem("xt_hi"), sem("xt_lo")
        c_sum, c_out = sem("c_sum"), sem("c_out")
        t_mm, t_hi, t_lo = sem("t_mm"), sem("t_hi"), sem("t_lo")
        t_st = [sem("t_st%d" % b) for b in range(2)]
        k_tr, k_hi, k_lo = sem("k_tr"), sem("k_hi"), sem("k_lo")
        v_tr, vt_hi, vt_lo = sem("v_tr"), sem("vt_hi"), sem("vt_lo")
        v_mm, vp_hi, vp_lo = sem("v_mm"), sem("vp_hi"), sem("vp_lo")
        kt_st, vp_st = sem("kt_st"), sem("vp_st")
        BA, BB, BC = 0, 2, 4
        NG = N // C

        def xT(slot, s):
            return VP[:, s, slot * KD:(slot + 1) * KD, :]

        def queries(slot, s):
            return VP[:, s, 2 * KD + slot * TC:2 * KD + (slot + 1) * TC, :]

        def transposes(bank, slot):
            for k in range(KD):
                last = nc.tensor.transpose(ps[:, bank, k * P:(k + 1) * P], rows[:, slot, k * P:(k + 1) * P], ident[:, :])
            return last

        def group_loop(eng, group):
            for b in range(2):
                group(b, b, True)
            with eng.Fori(1, NG // 2 - 1) as i:
                for b in range(2):
                    group(2 * i + b, b, True)
            for b in range(2):
                group(NG - 2 + b, b, b == 0)

        with nc.Block() as block:

            @block.sync
            def _(sp):
                for e in range(KD):
                    sp.dma_start(wa[:, e, :], wq[e * P:(e + 1) * P, :]).then_inc(s_w[e], 16)
                    sp.dma_start(wb[:, e, :], wk[e * P:(e + 1) * P, :]).then_inc(s_w[e], 16)
                with nc.allow_non_contiguous_dma(reason="three bias vectors, once"):
                    for n, b in enumerate((bq, bk, bv)):
                        sp.dma_start(bcol[:, n, :], b.rearrange("(k p) -> p k", p=P)).then_inc(s_bc, 16)
                sp.dma_start(bias_o[:, :], bm.rearrange("(a n) -> a n", a=1).to_broadcast([P, D])).then_inc(s_bm, 16)
                sp.dma_start(wc[:, :, :], wv.rearrange("(e p) d -> p e d", p=P)).then_inc(s_wv, 16)
                sp.dma_start(wd[:, :, :], wm.rearrange("(o p) e -> p o e", p=P)).then_inc(s_wm, 16)

                def x_loads(G):
                    for j in range(TC):
                        n = TC * G + j
                        wait(sp, x_tr, n - TC + 1)
                        wait(sp, c_sum, n - TC + 1)
                        sp.dma_start(rows[:, j, :], x[bass.ds(n * P, P), :]).then_inc(row_in[j], 16)

                def kv_loads(i, section):
                    half = (1 - section) * HALF
                    for b in range(2):
                        g = section * MT + 2 * i + b
                        wait(sp, k_tr, g - 1)
                        sp.dma_start(rows[:, b, :], key[bass.ds(half + (2 * i + b) * P, P), :]).then_inc(row_in[b], 16)
                        wait(sp, v_tr, g - 1)
                        sp.dma_start(rows[:, 2 + b, :], value[bass.ds(half + (2 * i + b) * P, P), :])\
                          .then_inc(row_in[2 + b], 16)

                x_loads(0)
                with sp.Fori(1, NG) as G:
                    x_loads(G)
                sp.wait_ge(x_tr, NT)
                sp.wait_ge(c_sum, NT)
                for section in range(2):
                    kv_loads(0, section)
                    with sp.Fori(1, MT // 2) as i:
                        kv_loads(i, section)

            @block.tensor
            def _(pe):
                def x_turn(G, j):
                    n = TC * G + j
                    pe.wait_ge(row_in[j], 16 * (G + 1))
                    wait(pe, xt_lo, n - 1)
                    transposes(BA + j % 2, j).then_inc(x_tr, 1)

                for e in range(KD):
                    pe.wait_ge(s_w[e], 32)
                    for d in range(KD):
                        last = nc.tensor.matmul(ps[:, d, :], wa[:, e, d * P:(d + 1) * P], wb[:, e, :],
                                                start=(e == 0), stop=(e == KD - 1))
                        if e == KD - 1:
                            last.then_inc(s_amm, 1)
                pe.wait_ge(s_rep, 3)
                for d in range(KD):
                    for e in range(KD):
                        last = nc.tensor.matmul(ps[:, 4, d:d + 1], wb[:, e, d * P:(d + 1) * P], bcol[:, 0, e:e + 1],
                                                start=(e == 0), stop=(e == KD - 1))
                last.then_inc(s_rmm, 1)
                for e in range(KD):
                    last = nc.tensor.matmul(ps[:, 5, :], brep[:, 1, e, :], wa[:, e, :],
                                            start=(e == 0), stop=(e == KD - 1))
                last.then_inc(s_rmm, 1)
                for e in range(KD):
                    last = nc.tensor.matmul(ps[:, 6, 0:1], brep[:, 0, e, :], bcol[:, 1, e:e + 1],
                                            start=(e == 0), stop=(e == KD - 1))
                last.then_inc(s_rmm, 1)
                pe.wait_ge(s_wm, 16)
                pe.wait_ge(s_wv, 16)
                pe.wait_ge(s_ident, 2)
                pe.wait_ge(s_alo, KD)
                for e in range(KD):
                    for o in range(KD):
                        last = nc.tensor.transpose(ps[:, e, o * P:(o + 1) * P], wd[:, o, e * P:(e + 1) * P], ident[:, :])
                    last.then_inc(s_wmt, 1)
                pe.wait_ge(s_wmc, KD)
                pe.wait_ge(s_rout, 3)
                for j in range(2):
                    x_turn(0, j)
                for d in range(KD):
                    for e in range(KD):
                        last = nc.tensor.matmul(ps[:, 4 + d, :], wc[:, e, d * P:(d + 1) * P], wmT[:, e, :],
                                                start=(e == 0), stop=(e == KD - 1))
                    last.then_inc(s_vmm, 1)
                    if d < 2:
                        x_turn(0, 2 + d)
                for e in range(KD):
                    last = nc.tensor.matmul(ps[:, 3, :], brep[:, 2, e, :], wmT[:, e, :],
                                            start=(e == 0), stop=(e == KD - 1))
                last.then_inc(s_bmm, 1)

                def query_features(G, b, e):
                    pe.wait_ge(xt_lo, TC * (G + 1))
                    wait(pe, t_lo, KD * (G - 1) + e + 1)
                    n = 0
                    for s, m in PASSES:
                        for k in range(KD):
                            last = nc.tensor.matmul(ps[:, BC + e, :], Aq[:, m, k, e * P:(e + 1) * P], xT(b, s)[:, k, :],
                                                    start=(n == 0), stop=(n == 3 * KD - 1))
                            n += 1
                    last.then_inc(t_mm, 1)

                def group(G, b, turn_next):
                    for e in range(KD):
                        if turn_next:
                            x_turn(G + 1, e)
                        query_features(G, b, e)

                def value_project(g, b):
                    pe.wait_ge(vt_lo, g + 1)
                    wait(pe, vp_lo, g - 1)
                    n = 0
                    for s, m in PASSES:
                        for k in range(KD):
                            last = nc.tensor.matmul(ps[:, BC + b, :], valueT[:, b, s, k * P:(k + 1) * P], Wvm[:, m, k, :],
                                                    start=(n == 0), stop=(n == 3 * KD - 1))
                            n += 1
                    last.then_inc(v_mm, 1)

                def kv_chunk(section, c):
                    for j in range(TC):
                        b = j % 2
                        g = section * MT + TC * c + j
                        pair = section * MT // 2 + TC // 2 * c + j // 2 + 1
                        pe.wait_ge(row_in[b], 16 * (NG + pair))
                        wait(pe, k_lo, g - 1)
                        transposes(BA + b, b).then_inc(k_tr, 1)
                        pe.wait_ge(row_in[2 + b], 16 * (NG + pair))
                        wait(pe, vt_lo, g - 1)
                        transposes(BB + b, 2 + b).then_inc(v_tr, 1)
                        if not (isinstance(g, int) and g == 0):
                            value_project(g - 1, 1 - b)

                pe.wait_ge(s_vlo, KD)
                group_loop(pe, group)
                pe.wait_ge(xt_lo, NT)
                pe.wait_ge(t_lo, KD * NG - 2)
                for section in range(2):
                    kv_chunk(section, 0)
                    with pe.Fori(1, MC) as c:
                        kv_chunk(section, c)
                value_project(NT - 1, 1)

            @block.scalar
            def _(act):
                def x_out(G, b, j):
                    act.wait_ge(x_tr, TC * G + j + 1)
                    wait(act, t_mm, KD * (G - 1))
                    nc.scalar.activation(xT(b, HI)[:, :, j * P:(j + 1) * P],
                                         ps[:, BA + j % 2, :].rearrange("p (k n) -> p k n", n=P),
                                         ACT.Copy).then_inc(xt_hi, 1)

                act.wait_ge(s_bc, 48)
                act.wait_ge(s_one, 1)
                for b in range(3):
                    for e in range(KD):
                        last = nc.scalar.activation(brep[:, b, e, :], ones[:, :], ACT.Copy, scale=bcol[:, b, e:e + 1])
                    last.then_inc(s_rep, 1)
                for d in range(KD):
                    act.wait_ge(s_amm, d + 1)
                    nc.scalar.activation(Aq[:, HI, d, :], ps[:, d, :], ACT.Copy, scale=SCALE).then_inc(s_ahi, 1)
                for e in range(KD):
                    act.wait_ge(s_wmt, e + 1)
                    nc.scalar.activation(wmT[:, e, :], ps[:, e, :], ACT.Copy).then_inc(s_wmc, 1)
                for j in range(2):
                    x_out(0, 0, j)
                for d in range(KD):
                    act.wait_ge(s_vmm, d + 1)
                    nc.scalar.activation(Wvm[:, HI, d, :], ps[:, 4 + d, :], ACT.Copy).then_inc(s_vhi, 1)
                    if d < 2:
                        x_out(0, 0, 2 + d)

                def group(G, b, turn_next):
                    for e in range(KD):
                        if turn_next:
                            x_out(G + 1, 1 - b, e)
                        act.wait_ge(t_mm, KD * G + e + 1)
                        if not isinstance(G, int) or G >= 2:
                            act.wait_ge(t_st[b], 8 * TC * (G - b))
                        nc.scalar.activation(queries(b, HI)[:, :, e * P:(e + 1) * P],
                                             ps[:, BC + e, :].rearrange("p (j n) -> p j n", n=P),
                                             ACT.Identity, bias=bq_k[:, e:e + 1]).then_inc(t_hi, 1)

                def value_out(g, tile, b):
                    act.wait_ge(v_mm, g + 1)
                    nc.scalar.activation(VP[:, HI, tile, :], ps[:, BC + b, :], ACT.Copy).then_inc(vp_hi, 1)

                def kv_chunk(section, c):
                    if section == 1:
                        act.wait_ge(kt_st, 16 * 2 * KD * (c + 1))
                        act.wait_ge(vp_st, 16 * TC * (c + 1))
                    for j in range(TC):
                        b = j % 2
                        tile = TC * c + j
                        g = section * MT + tile
                        act.wait_ge(k_tr, g + 1)
                        nc.scalar.activation(KT[:, HI, :, bass.ts(tile, P)],
                                             ps[:, BA + b, :].rearrange("p (k n) -> p k n", n=P),
                                             ACT.Copy).then_inc(k_hi, 1)
                        act.wait_ge(v_tr, g + 1)
                        wait(act, v_mm, g - 1)
                        nc.scalar.activation(valueT[:, b, HI, :], ps[:, BB + b, :], ACT.Copy).then_inc(vt_hi, 1)
                        if not isinstance(tile, int) or tile > 0:
                            value_out(g - 1, tile - 1, 1 - b)
                        elif section == 1:
                            value_out(g - 1, MT - 1, 1 - b)

                group_loop(act, group)
                for section in range(2):
                    kv_chunk(section, 0)
                    if section == 0:
                        for b in range(2):
                            act.wait_ge(t_st[b], 8 * TC * NG)
                    with act.Fori(1, MC) as c:
                        kv_chunk(section, c)
                value_out(NT - 1, MT - 1, 1)

            @block.vector
            def _(dve):
                def x_out(G, b, j):
                    n = TC * G + j
                    dve.wait_ge(xt_hi, n + 1)
                    nc.vector.tensor_tensor(xT(b, LO)[:, :, j * P:(j + 1) * P],
                                            ps[:, BA + j % 2, :].rearrange("p (k n) -> p k n", n=P),
                                            xT(b, HI)[:, :, j * P:(j + 1) * P].bitcast(fp32),
                                            ALU.subtract).then_inc(xt_lo, 1)
                    wait(dve, c_out, n - 1)
                    nc.vector.tensor_tensor_reduce(out=xu[:, :], in0=rows[:, j, :], in1=bk_q[:, :], scale=1.0,
                                                   scalar=bqbk[:, 0:1], op0=ALU.mult, op1=ALU.add,
                                                   accum_out=c_tmp[:, j % 2:j % 2 + 1]).then_inc(c_sum, 1)

                def c_keep(n, b):
                    dve.wait_ge(c_sum, n + 1)
                    nc.vector.tensor_copy(c_all[:, bass.ds(n, 1)], c_tmp[:, b:b + 1]).then_inc(c_out, 1)

                for d in range(KD):
                    dve.wait_ge(s_ahi, d + 1)
                    nc.vector.scalar_tensor_tensor(out=Aq[:, LO, d, :], in0=ps[:, d, :], scalar=SCALE,
                                                   in1=Aq[:, HI, d, :].bitcast(fp32), op0=ALU.mult,
                                                   op1=ALU.subtract).then_inc(s_alo, 1)
                dve.wait_ge(s_rmm, 3)
                nc.vector.tensor_scalar(bq_k[:, :], ps[:, 4, 0:KD], SCALE, None, ALU.mult).then_inc(s_rout, 1)
                nc.vector.tensor_scalar(bk_q[:, :], ps[:, 5, :], SCALE, None, ALU.mult).then_inc(s_rout, 1)
                nc.vector.tensor_scalar(bqbk[:, :], ps[:, 6, 0:1], SCALE, None, ALU.mult).then_inc(s_rout, 1)
                for j in range(2):
                    x_out(0, 0, j)
                    c_keep(j, j)
                for d in range(KD):
                    dve.wait_ge(s_vhi, d + 1)
                    nc.vector.tensor_tensor(Wvm[:, LO, d, :], ps[:, 4 + d, :], Wvm[:, HI, d, :].bitcast(fp32),
                                            ALU.subtract).then_inc(s_vlo, 1)
                    if d < 2:
                        x_out(0, 0, 2 + d)
                        c_keep(2 + d, d)
                dve.wait_ge(s_bmm, 1)
                dve.wait_ge(s_bm, 16)
                nc.vector.tensor_tensor(bias_o[:, :], ps[:, 3, :], bias_o[:, :], ALU.add).then_inc(s_bout, 1)

                def group(G, b, turn_next):
                    for e in range(KD):
                        if turn_next:
                            x_out(G + 1, 1 - b, e)
                        dve.wait_ge(t_hi, KD * G + e + 1)
                        nc.vector.scalar_tensor_tensor(out=queries(b, LO)[:, :, e * P:(e + 1) * P],
                                                       in0=ps[:, BC + e, :].rearrange("p (j n) -> p j n", n=P),
                                                       scalar=bq_k[:, e:e + 1],
                                                       in1=queries(b, HI)[:, :, e * P:(e + 1) * P].bitcast(fp32),
                                                       op0=ALU.add, op1=ALU.subtract).then_inc(t_lo, 1)
                        if turn_next:
                            c_keep(TC * (G + 1) + e, e % 2)

                def value_out(g, tile, b):
                    dve.wait_ge(vp_hi, g + 1)
                    nc.vector.tensor_tensor(VP[:, LO, tile, :], ps[:, BC + b, :], VP[:, HI, tile, :].bitcast(fp32),
                                            ALU.subtract).then_inc(vp_lo, 1)

                def kv_chunk(section, c):
                    for j in range(TC):
                        b = j % 2
                        tile = TC * c + j
                        g = section * MT + tile
                        dve.wait_ge(k_hi, g + 1)
                        nc.vector.tensor_tensor(KT[:, LO, :, bass.ts(tile, P)],
                                                ps[:, BA + b, :].rearrange("p (k n) -> p k n", n=P),
                                                KT[:, HI, :, bass.ts(tile, P)].bitcast(fp32),
                                                ALU.subtract).then_inc(k_lo, 1)
                        dve.wait_ge(vt_hi, g + 1)
                        nc.vector.tensor_tensor(valueT[:, b, LO, :], ps[:, BB + b, :], valueT[:, b, HI, :].bitcast(fp32),
                                                ALU.subtract).then_inc(vt_lo, 1)
                        if not isinstance(tile, int) or tile > 0:
                            value_out(g - 1, tile - 1, 1 - b)
                        elif section == 1:
                            value_out(g - 1, MT - 1, 1 - b)

                group_loop(dve, group)
                for section in range(2):
                    kv_chunk(section, 0)
                    with dve.Fori(1, MC) as c:
                        kv_chunk(section, c)
                value_out(NT - 1, MT - 1, 1)

            @block.gpsimd
            def _(pool):
                nc.gpsimd.memset(ident[:, :], 0.0).then_inc(s_ident, 1)
                nc.gpsimd.memset(ones[:, :], 1.0).then_inc(s_one, 1)
                pool.wait_ge(s_ident, 1)
                nc.gpsimd.affine_select(out=ident[:, :], in_=ident[:, :], compare_op=ALU.not_equal, fill=1.0,
                                        base=0, pattern=[[-1, P]], channel_multiplier=1).then_inc(s_ident, 1)

                with pool.Fori(0, NG // 2) as i:
                    for b in range(2):
                        G = 2 * i + b
                        pool.wait_ge(t_lo, KD * (G + 1))
                        for j in range(TC):
                            tile = 2 * KD + b * TC + j
                            pool.dma_start(t_dram[bass.ds(TC * G + j, 1), :, :].rearrange("a p (s d) -> p s (a d)", s=2),
                                           VP[:, :, tile, :].bitcast(fp32)).then_inc(t_st[b], 16)
                for c in range(MC):
                    wait(pool, kt_st, 16 * 2 * KD * c)
                    wait(pool, vp_st, 16 * TC * c)
                    pool.wait_ge(k_lo, TC * (c + 1))
                    for s in (HI, LO):
                        for k in range(KD):
                            pool.dma_start(kt_dram[:, s, k, c * C:(c + 1) * C],
                                           KT[:, s, k, c * C:(c + 1) * C].bitcast(fp32)).then_inc(kt_st, 16)
                    pool.wait_ge(vp_lo, TC * (c + 1))
                    for m in range(c * TC, (c + 1) * TC):
                        pool.dma_start(vp_dram[:, :, m, :], VP[:, :, m, :].bitcast(fp32)).then_inc(vp_st, 16)
                pool.wait_ge(kt_st, 16 * 2 * KD * MC)
                pool.wait_ge(vp_st, 16 * MT)

        work.close()
        prep.close()

        work = ExitStack()
        adj_rows = sb(work, "adj_rows", [P, 2, HALF], fp32)
        prob = sb(work, "prob", [P, 2, HALF], fp32)
        small = sb(work, "small", [P, 2, C], fp32)
        t_in = sb(work, "t_in", [P, 2, 2, D], f32r)
        probT = sb(work, "probT", [P, 2, 2, C], f32r)
        x_in = sb(work, "x_in", [P, 2, D], fp32)
        o_in = sb(work, "o_in", [P, 2, D], fp32)
        z_out = sb(work, "z_out", [P, 2, D], fp32)
        chunk_max = sb(work, "chunk_max", [P, 2, MC], fp32)
        nmax = sb(work, "nmax", [P, 2], fp32)
        rsum = sb(work, "rsum", [P, 2], fp32)
        nm_pair = sb(work, "nm_pair", [P, 2, 2], fp32)
        ls_pair = sb(work, "ls_pair", [P, 2, 2], fp32)
        nm = sb(work, "nm", [P, 2], fp32)
        wgt = sb(work, "wgt", [P, 2, 2], fp32)
        wls = sb(work, "wls", [P, 2, 2], fp32)
        den = sb(work, "den", [P, 2], fp32)
        rden = sb(work, "rden", [P, 2], fp32)
        wn = sb(work, "wn", [P, 2, 2], fp32)
        bst = sb(work, "bst", [P, 2, 6], fp32)
        mv = sb(work, "mv", [P, 2, 2], fp32)
        c_now = sb(work, "c_now", [P, 2], fp32)
        adj_in = [sem("adj_in%d" % b) for b in range(2)]
        q_in = [sem("q_in%d" % b) for b in range(2)]
        xo_in = [sem("xo_in%d" % b) for b in range(2)]
        kt_in = [sem("kt_in%d" % c) for c in range(MC)]
        vp_in = [sem("vp_in%d" % c) for c in range(MC)]
        s_mm, s_adj, s_abs, s_neg, s_mask = [sem(n) for n in ("s_mm", "s_adj", "s_abs", "s_neg", "s_mask")]
        s_max, s_exp, s_keep, s_c = sem("s_max"), sem("s_exp"), sem("s_keep"), sem("s_c")
        p_use, s_mv = sem("p_use"), sem("s_mv")
        p_tr, p_hi, p_lo, o_mm = [sem(n) for n in ("p_tr", "p_hi", "p_lo", "o_mm")]
        ab_st = [sem("ab_st%d" % b) for b in range(2)]
        o_out = sem("o_out")
        o_st = [sem("o_st%d" % b) for b in range(2)]
        m_step, m_w, xb = sem("m_step"), sem("m_w"), sem("xb")
        BS, BP, BO = 0, 4, 6

        with nc.Block() as block:

            @block.sync
            def _(sp):
                def loads(g, n, b, half):
                    wait(sp, s_mm, MC * (g - 1))
                    sp.dma_start(t_in[:, b, :, :].rearrange("p s d -> p (s d)").bitcast(fp32), t_dram[n, :, :])\
                      .then_inc(q_in[b], 16)
                    if not isinstance(g, int) or g >= 2:
                        sp.wait_ge(ab_st[b], 8 * (g - b))
                    sp.dma_start(adj_rows[:, b, :], adj[bass.ds(n * P, P), half * HALF:(half + 1) * HALF])\
                      .then_inc(adj_in[b], 16)

                def loads_x_o(n, b):
                    sp.dma_start(x_in[:, b, :], x[bass.ds(n * P, P), :]).then_inc(xo_in[b], 16)
                    sp.dma_start(o_in[:, b, :], o_dram[bass.ds(n * P, P), :]).then_inc(xo_in[b], 16)

                def store(g, n, b, half):
                    sp.wait_ge(o_out, g + 1)
                    dst = z_dram if half == 1 else o_dram
                    sp.dma_start(dst[bass.ds(n * P, P), :], z_out[:, b, :]).then_inc(o_st[b], 16)

                for n in range(3):
                    loads(n, n, n % 2, 0)
                with sp.Fori(1, NT // 2 - 1) as i:
                    for b in range(2):
                        loads(2 * i + b + 1, 2 * i + b + 1, 1 - b, 0)
                        store(2 * i + b - 2, 2 * i + b - 2, b, 0)
                loads(NT - 1, NT - 1, 1, 0)
                for n in (NT - 4, NT - 3):
                    store(n, n, n % 2, 0)
                for c in range(MC):
                    sp.wait_ge(s_mm, MC * (NT - 1) + c + 1)
                    sp.dma_start(KT[:, :, :, c * C:(c + 1) * C].rearrange("p s k n -> p (s k) n").bitcast(fp32),
                                 kt_dram[:, :, :, c * C:(c + 1) * C].rearrange("p s k n -> p (s k) n"))\
                      .then_inc(kt_in[c], 16)
                loads(NT, 0, 0, 1)
                store(NT - 2, NT - 2, 0, 0)
                loads(NT + 1, 1, 1, 1)
                sp.wait_ge(o_mm, NT)
                for c in range(MC):
                    if c == 2:
                        loads(NT + 2, 2, 0, 1)
                    sp.dma_start(VP[:, :, c * TC:(c + 1) * TC, :].bitcast(fp32),
                                 vp_dram[:, :, c * TC:(c + 1) * TC, :]).then_inc(vp_in[c], 16)
                store(NT - 1, NT - 1, 1, 0)
                for b in range(2):
                    sp.wait_ge(o_st[b], 16 * (NT // 2))
                for b in range(2):
                    loads_x_o(b, b)
                with sp.Fori(1, NT // 2 - 1) as i:
                    for b in range(2):
                        loads(NT + 2 * i + b + 1, 2 * i + b + 1, 1 - b, 1)
                        store(NT + 2 * i + b - 2, 2 * i + b - 2, b, 1)
                        loads_x_o(2 * i + b, b)
                loads(2 * NT - 1, NT - 1, 1, 1)
                for n in (NT - 4, NT - 3):
                    store(NT + n, n, n % 2, 1)
                    loads_x_o(n + 2, n % 2)
                for b in range(2):
                    store(2 * NT - 2 + b, NT - 2 + b, b, 1)
                for b in range(2):
                    sp.wait_ge(o_st[b], 16 * NT)

            @block.gpsimd
            def _(pool):
                for half in range(2):
                    with pool.Fori(0, NT // 2) as i:
                        for b in range(2):
                            pool.wait_ge(s_adj, MC * (half * NT + 2 * i + b + 1))
                            pool.dma_start(adj_bf[bass.ds((2 * i + b) * P, P), half * HALF:(half + 1) * HALF],
                                           adj_rows[:, b, :]).then_inc(ab_st[b], 16)
                for b in range(2):
                    pool.wait_ge(ab_st[b], 16 * NT)

            @block.tensor
            def _(pe):
                def scores(g, b, c):
                    wait(pe, s_adj, MC * (g - 1) + c + 1)
                    n = 0
                    for s, m in PASSES:
                        for k in range(KD):
                            last = nc.tensor.matmul(ps[:, BS + c, :], t_in[:, b, s, k * P:(k + 1) * P],
                                                    KT[:, m, k, c * C:(c + 1) * C],
                                                    start=(n == 0), stop=(n == 3 * KD - 1))
                            n += 1
                    last.then_inc(s_mm, 1)

                def turn(g, b, r):
                    if r == 0:
                        pe.wait_ge(s_exp, g + 1)
                    wait(pe, p_lo, MC * g + r - 1)
                    for j in range(TC):
                        m = r * TC + j
                        last = nc.tensor.transpose(ps[:, BP + r % 2, j * P:(j + 1) * P],
                                                   prob[:, b, m * P:(m + 1) * P], ident[:, :])
                    last.then_inc(p_tr, 1)

                def weigh(g, b, r):
                    if r == 0:
                        wait(pe, o_out, g - 1)
                    pe.wait_ge(p_lo, MC * g + r + 1)
                    for j in range(TC):
                        m = r * TC + j
                        for q, (s, v) in enumerate(PASSES):
                            last = nc.tensor.matmul(ps[:, BO + b, :], probT[:, r % 2, s, j * P:(j + 1) * P], VP[:, v, m, :],
                                                    start=(m == 0 and q == 0), stop=(m == MT - 1 and q == 2))
                    last.then_inc(o_mm, 1) if r == MC - 1 else last.then_inc(p_use, 1)

                def step(g, b, i, half, make, use):
                    if make:
                        pe.wait_ge(q_in[b], 16 * (half * NT // 2 + i + 1))
                    for c in range(MC):
                        if make:
                            if half == 1 and not use:
                                pe.wait_ge(kt_in[c], 16)
                            scores(g, b, c)
                        if use and c in (1, 2):
                            turn(g - 1, 1 - b, c - 1)
                    if use:
                        for r in range(MC):
                            if half == 1 and isinstance(i, int) and i == 0:
                                pe.wait_ge(vp_in[r], 16)
                            weigh(g - 1, 1 - b, r)
                            if r + 2 < MC:
                                turn(g - 1, 1 - b, r + 2)

                for half in range(2):
                    g0 = half * NT
                    step(g0, 0, 0, half, True, False)
                    step(g0 + 1, 1, 0, half, True, True)
                    for b in range(2):
                        step(g0 + 2 + b, b, 1, half, True, True)
                    with pe.Fori(2, NT // 2) as i:
                        for b in range(2):
                            step(g0 + 2 * i + b, b, i, half, True, True)
                    step(g0 + NT, 0, None, half, False, True)

            @block.scalar
            def _(act):
                def magnitude(g, b, c):
                    act.wait_ge(s_adj, MC * g + c + 1)
                    wait(act, s_mask, MC * g + c - 1)
                    nc.scalar.activation(small[:, c % 2, :], prob[:, b, c * C:(c + 1) * C], ACT.Abs).then_inc(s_abs, 1)

                def exponentials(g, b):
                    act.wait_ge(s_max, g + 1)
                    wait(act, s_keep, g - 1)
                    nc.scalar.activation(prob[:, b, :], prob[:, b, :], ACT.Exp, bias=nmax[:, b:b + 1],
                                         accum_out=rsum[:, b:b + 1]).then_inc(s_exp, 1)

                def turned(g, r):
                    act.wait_ge(p_tr, MC * g + r + 1)
                    slot_free(g, r)
                    nc.scalar.activation(probT[:, r % 2, HI, :], ps[:, BP + r % 2, :], ACT.Copy).then_inc(p_hi, 1)

                def slot_free(g, r):
                    if r >= 2:
                        act.wait_ge(p_use, (MC - 1) * g + r - 1)
                    elif r == 1:
                        wait(act, o_mm, g)
                    else:
                        wait(act, p_use, (MC - 1) * g)

                def step(g, b, half, make, use, merge):
                    for c in range(MC):
                        if make:
                            magnitude(g, b, c)
                        if use and c in (1, 2):
                            turned(g - 1, c - 1)
                        if merge and c == 1:
                            finish(g - 2, b, half)
                    if use:
                        turned(g - 1, 2)
                        turned(g - 1, 3)
                    if make:
                        exponentials(g, b)

                def finish(g, b, half):
                    if half == 0:
                        act.wait_ge(o_mm, g + 1)
                        if not isinstance(g, int) or g >= 2:
                            act.wait_ge(o_st[b], 8 * (g - b))
                        nc.scalar.activation(z_out[:, b, :], ps[:, BO + b, :], ACT.Copy).then_inc(o_out, 1)
                    else:
                        act.wait_ge(m_w, 2 * (g - NT) + 1)
                        nc.scalar.activation(wgt[:, b, :], nm_pair[:, b, :], ACT.Exp, bias=nm[:, b:b + 1],
                                             scale=-1.0).then_inc(m_w, 1)

                for half in range(2):
                    g0 = half * NT
                    step(g0, 0, half, True, False, False)
                    step(g0 + 1, 1, half, True, True, False)
                    for b in range(2):
                        step(g0 + 2 + b, b, half, True, True, True)
                    with act.Fori(2, NT // 2) as i:
                        for b in range(2):
                            step(g0 + 2 * i + b, b, half, True, True, True)
                    step(g0 + NT, 0, half, False, True, True)
                    finish(g0 + NT - 1, 1, half)

            @block.vector
            def _(dve):
                def masked(g, b, c, i, half):
                    if c == 0:
                        dve.wait_ge(adj_in[b], 16 * (half * NT // 2 + i + 1))
                        wait(dve, p_tr, MC * (g - 1))
                        nc.vector.tensor_copy(c_now[:, b:b + 1], c_all[:, bass.ds(2 * i + b, 1)]).then_inc(s_c, 1)
                        dve.wait_ge(s_c, g + 1)
                    dve.wait_ge(s_mm, MC * g + c + 1)
                    nc.vector.scalar_tensor_tensor(out=prob[:, b, c * C:(c + 1) * C], in0=ps[:, BS + c, :],
                                                   scalar=c_now[:, b:b + 1], in1=adj_rows[:, b, c * C:(c + 1) * C],
                                                   op0=ALU.add, op1=ALU.mult).then_inc(s_adj, 1)

                def small_scores(g, b, c):
                    dve.wait_ge(s_abs, MC * g + c + 1)
                    nc.vector.tensor_scalar(small[:, c % 2, :], small[:, c % 2, :], EPS_SCORE, MASKED,
                                            ALU.is_lt, ALU.mult).then_inc(s_neg, 1)

                def small_ready(g, c):
                    dve.wait_ge(s_neg, MC * g + c + 1)

                def threshold(b, c):
                    nc.vector.tensor_tensor_reduce(out=prob[:, b, c * C:(c + 1) * C], in0=prob[:, b, c * C:(c + 1) * C],
                                                   in1=small[:, c % 2, :], scale=1.0, scalar=-3.4e38, op0=ALU.add,
                                                   op1=ALU.max, accum_out=chunk_max[:, b, c:c + 1]).then_inc(s_mask, 1)

                def maximum(g, b, n, half):
                    dve.wait_ge(s_mask, MC * (g + 1))
                    wait(dve, s_exp, g - 1)
                    nc.vector.tensor_reduce(nmax[:, b:b + 1], chunk_max[:, b, :], AX.X, ALU.max, negate=True)\
                             .then_inc(s_max, 1)

                def keep_maximum(g, b, n, half):
                    dve.wait_ge(s_max, g + 1)
                    nc.vector.tensor_copy(neg_max[:, bass.ds(n, 1), half], nmax[:, b:b + 1])

                def keep_sum(g, b, n, half):
                    dve.wait_ge(s_exp, g + 1)
                    nc.vector.tensor_copy(row_sum[:, bass.ds(n, 1), half], rsum[:, b:b + 1]).then_inc(s_keep, 1)

                def turned(g, r):
                    dve.wait_ge(p_hi, MC * g + r + 1)
                    nc.vector.tensor_tensor(probT[:, r % 2, LO, :], ps[:, BP + r % 2, :],
                                            probT[:, r % 2, HI, :].bitcast(fp32), ALU.subtract).then_inc(p_lo, 1)

                def pick(g, b, n):
                    k = g - NT
                    nc.vector.tensor_copy(nm_pair[:, b, :], neg_max[:, bass.ds(n, 1), :].rearrange("p a h -> p (a h)"))
                    nc.vector.tensor_copy(ls_pair[:, b, :], row_sum[:, bass.ds(n, 1), :].rearrange("p a h -> p (a h)"))\
                             .then_inc(m_step, 1)
                    dve.wait_ge(m_step, 7 * k + 1)
                    nc.vector.tensor_reduce(nm[:, b:b + 1], nm_pair[:, b, :], AX.X, ALU.min).then_inc(m_w, 1)

                def merge(g, b, i):
                    k = g - NT
                    dve.wait_ge(m_w, 2 * k + 2)
                    nc.vector.tensor_tensor(wls[:, b, :], wgt[:, b, :], ls_pair[:, b, :], ALU.mult).then_inc(m_step, 1)
                    dve.wait_ge(m_step, 7 * k + 2)
                    nc.vector.reduce_sum(den[:, b:b + 1], wls[:, b, :], AX.X).then_inc(m_step, 1)
                    dve.wait_ge(m_step, 7 * k + 3)
                    nc.vector.reciprocal(rden[:, b:b + 1], den[:, b:b + 1]).then_inc(m_step, 1)
                    dve.wait_ge(m_step, 7 * k + 4)
                    nc.vector.tensor_scalar(wn[:, b, :], wgt[:, b, :], rden[:, b:b + 1], None, ALU.mult).then_inc(m_step, 1)
                    dve.wait_ge(xo_in[b], 32 * (i + 1))
                    dve.wait_ge(o_st[b], 16 * (NT // 2 + i))
                    nc.vector.tensor_tensor(x_in[:, b, :], x_in[:, b, :], bias_o[:, :], ALU.add).then_inc(xb, 1)
                    dve.wait_ge(m_step, 7 * k + 5)
                    dve.wait_ge(xb, k + 1)
                    nc.vector.scalar_tensor_tensor(out=x_in[:, b, :], in0=o_in[:, b, :], scalar=wn[:, b, 0:1],
                                                   in1=x_in[:, b, :], op0=ALU.mult, op1=ALU.add).then_inc(m_step, 1)
                    dve.wait_ge(o_mm, g + 1)
                    dve.wait_ge(m_step, 7 * k + 6)
                    nc.vector.scalar_tensor_tensor(out=z_out[:, b, :], in0=ps[:, BO + b, :], scalar=wn[:, b, 1:2],
                                                   in1=x_in[:, b, :], op0=ALU.mult, op1=ALU.add).then_inc(o_out, 1)
                    dve.wait_ge(o_out, g + 1)
                    nc.vector.bn_stats(bst[:, b, :], z_out[:, b, :]).then_inc(m_step, 1)

                def row_stats(g, b, n):
                    k = g - NT
                    nc.vector.bn_aggr(mv[:, b, :], bst[:, b, :]).then_inc(s_mv, 1)
                    dve.wait_ge(s_mv, k + 1)
                    nc.vector.tensor_copy(stats[:, bass.ds(n, 1), :].rearrange("p a h -> p (a h)"), mv[:, b, :])

                def step(g, b, i, half, make, use, fin):
                    n = None if i is None else 2 * i + b
                    fin = fin and half == 1
                    if use:
                        keep_sum(g - 1, 1 - b, (NT if n is None else n) - 1, half)
                    if fin:
                        pick(g - 2, b, (NT if n is None else n) - 2)
                    if make:
                        masked(g, b, 0, i, half)
                        masked(g, b, 1, i, half)
                        small_scores(g, b, 0)
                        small_ready(g, 0)
                    if use:
                        turned(g - 1, 0)
                    if make:
                        threshold(b, 0)
                    if make:
                        masked(g, b, 2, i, half)
                        small_scores(g, b, 1)
                        small_ready(g, 1)
                    if use:
                        turned(g - 1, 1)
                    if make:
                        threshold(b, 1)
                        masked(g, b, 3, i, half)
                        small_scores(g, b, 2)
                        small_ready(g, 2)
                        small_scores(g, b, 3)
                        threshold(b, 2)
                        small_ready(g, 3)
                    if use:
                        turned(g - 1, 2)
                    if make:
                        threshold(b, 3)
                        maximum(g, b, n, half)
                    if use:
                        turned(g - 1, 3)
                    if fin:
                        merge(g - 2, b, (NT // 2 if i is None else i) - 1)
                        dve.wait_ge(m_step, 7 * (g - 2 - NT) + 7)
                    if make:
                        keep_maximum(g, b, n, half)
                    if fin:
                        row_stats(g - 2, b, (NT if n is None else n) - 2)

                for half in range(2):
                    g0 = half * NT
                    step(g0, 0, 0, half, True, False, False)
                    step(g0 + 1, 1, 0, half, True, True, False)
                    for b in range(2):
                        step(g0 + 2 + b, b, 1, half, True, True, True)
                    with dve.Fori(2, NT // 2) as i:
                        for b in range(2):
                            step(g0 + 2 * i + b, b, i, half, True, True, True)
                    step(g0 + NT, 0, None, half, False, True, True)
                    if half == 1:
                        pick(g0 + NT - 1, 1, NT - 1)
                        merge(g0 + NT - 1, 1, NT // 2 - 1)
                        dve.wait_ge(m_step, 7 * NT)
                        row_stats(g0 + NT - 1, 1, NT - 1)

        work.close()
        resident.close()

        work = ExitStack()
        WT = sb(work, "WT", [P, 2, KD, D], f32r)
        X1 = sb(work, "X1", [P, 2, NT, D], fp16)
        b1_rep = sb(work, "b1_rep", [P, D], fp32)
        w_raw = sb(work, "w_raw", [P, KD, D], fp32)
        z_in = sb(work, "z_in", [P, 2, TC, D], fp32)
        std = sb(work, "std", [P, NT, 1], fp32)
        rstd = sb(work, "rstd", [P, NT, 1], fp32)
        QUARTER = N // 4
        QT = QUARTER // P
        adjT = sb(work, "adjT", [P, 4, QT, C], bf16)
        G = sb(work, "G", [P, 2, KD, C], f32r)
        zf = sb(work, "zf", [P, 2, D], fp32)
        y = sb(work, "y", [P, 2, D], fp32)
        res = sb(work, "res", [P, 2, D], fp32)
        bst2 = sb(work, "bst2", [P, 2, 6], fp32)
        mv2 = sb(work, "mv2", [P, 2, 2], fp32)
        vare = sb(work, "vare", [P, 2], fp32)
        std2 = sb(work, "std2", [P, 2], fp32)
        rstd2 = sb(work, "rstd2", [P, 2], fp32)
        st_now = sb(work, "st_now", [P, 2, 3], fp32)
        w_in, b1_in, n_var, n_std, n_rstd = [sem(n) for n in ("w_in", "b1_in", "n_var", "n_std", "n_rstd")]
        zg_in = [sem("zg_in%d" % b) for b in range(2)]
        x1_full, x1_hi, x1_lo = sem("x1_full"), sem("x1_hi"), sem("x1_lo")
        w_tr, w_hi, w_lo = sem("w_tr"), sem("w_hi"), sem("w_lo")
        aq_in = [sem("aq_in%d" % q) for q in range(4)]
        a_use = sem("a_use")
        g_mm, g_hi, g_lo = sem("g_mm"), sem("g_hi"), sem("g_lo")
        f_mm, f_out = sem("f_mm"), sem("f_out")
        zf_in = [sem("zf_in%d" % b) for b in range(2)]
        f_x1, f_sum, f_bn = sem("f_x1"), sem("f_sum"), sem("f_bn")
        f_var, f_std, f_res = sem("f_var"), sem("f_std"), sem("f_res")
        f_mv, f_rstd = sem("f_mv"), sem("f_rstd")
        out_st = [sem("out_st%d" % b) for b in range(2)]
        BG, BF = 0, 6
        NB = N // C
        FIRST_F, NEXT_F = 2, 3

        with nc.Block() as block:

            @block.sync
            def _(sp):
                def z_group(i, b):
                    wait(sp, x1_lo, TC * (2 * i + b - 1))
                    sp.dma_start(z_in[:, b, :, :],
                                 z_dram[bass.ds((2 * i + b) * C, C), :].rearrange("(k p) d -> p k d", p=P))\
                      .then_inc(zg_in[b], 16)

                def adj_quarter(nb, q):
                    sp.dma_start_transpose(adjT[:, q, :, :], adj_bf[bass.ds(nb * C, C), q * QUARTER:(q + 1) * QUARTER])\
                      .then_inc(aq_in[q], 16)

                for i in range(NB // 2):
                    for b in range(2):
                        z_group(i, b)
                        if b == 0:
                            adj_quarter(0, i)
                    if i == 0:
                        sp.dma_start(w_raw[:, :, :], w1.rearrange("(o p) e -> p o e", p=P)).then_inc(w_in, 16)
                        sp.dma_start(b1_rep[:, :], b1.rearrange("(a n) -> a n", a=1).to_broadcast([P, D])).then_inc(b1_in, 16)
                with sp.Fori(1, NB) as nb:
                    for q in range(4):
                        if q < 3:
                            sp.wait_ge(a_use, 3 * (nb - 1) + q + 1)
                        else:
                            sp.wait_ge(g_mm, KD * nb)
                        adj_quarter(nb, q)

            @block.tensor
            def _(pe):
                def second_weights():
                    pe.wait_ge(w_in, 16)
                    for e in range(KD):
                        for o in range(KD):
                            last = nc.tensor.transpose(ps[:, 4 + e, o * P:(o + 1) * P], w_raw[:, o, e * P:(e + 1) * P],
                                                       ident[:, :])
                        last.then_inc(w_tr, 1)

                def aggregate(nb, m):
                    q = m // QT
                    if m % QT == 0:
                        pe.wait_ge(aq_in[q], 16 * (nb + 1))
                    for d in range(KD):
                        if m == 0:
                            wait(pe, g_lo, KD * (nb - 1) + d + 1)
                        for s in (HI, LO):
                            last = nc.tensor.matmul(ps[:, BG + d, :], X1[:, s, m, d * P:(d + 1) * P], adjT[:, q, m % QT, :],
                                                    start=(m == 0 and s == HI), stop=(m == NT - 1 and s == LO))
                        if m == NT - 1:
                            last.then_inc(g_mm, 1)
                    if m % QT == QT - 1 and m < NT - 1:
                        last.then_inc(a_use, 1)

                def output(nb, k):
                    pe.wait_ge(g_lo, KD * (nb + 1))
                    wait(pe, f_out, TC * nb + max(k - 1, 0))
                    n = 0
                    for s, w in PASSES:
                        for d in range(KD):
                            last = nc.tensor.matmul(ps[:, BF + k % 2, :], G[:, s, d, k * P:(k + 1) * P], WT[:, w, d, :],
                                                    start=(n == 0), stop=(n == 3 * KD - 1))
                            n += 1
                    last.then_inc(f_mm, 1)

                def rows(nb, outputs):
                    for m in range(NT):
                        if outputs is None:
                            pe.wait_ge(x1_lo, m + 1)
                            if m == QT:
                                second_weights()
                        aggregate(nb, m)
                        if outputs is not None and m >= FIRST_F and (m - FIRST_F) % NEXT_F == 0 \
                                and (m - FIRST_F) // NEXT_F < TC:
                            output(outputs, (m - FIRST_F) // NEXT_F)

                rows(0, None)
                pe.wait_ge(w_lo, KD)
                rows(1, 0)
                with pe.Fori(2, NB) as nb:
                    rows(nb, nb - 1)
                for k in range(TC):
                    output(NB - 1, k)

            @block.scalar
            def _(act):
                act.wait_ge(n_var, 1)
                nc.scalar.activation(std[:, :, :], std[:, :, :], ACT.Sqrt).then_inc(n_std, 1)
                def x1_tiles(i):
                    for b in range(2):
                        for k in range(TC):
                            n = TC * (2 * i + b) + k
                            act.wait_ge(x1_full, n + 1)
                            nc.scalar.activation(X1[:, HI, bass.ds(n, 1), :].rearrange("p a d -> p (a d)"),
                                                 z_in[:, b, k, :], ACT.Copy).then_inc(x1_hi, 1)

                with act.Fori(0, NB // 2) as i:
                    x1_tiles(i)
                for e in range(KD):
                    act.wait_ge(w_tr, e + 1)
                    nc.scalar.activation(WT[:, HI, e, :], ps[:, 4 + e, :], ACT.Copy).then_inc(w_hi, 1)

                def root(nb, k):
                    act.wait_ge(f_var, TC * nb + k + 1)
                    nc.scalar.activation(std2[:, k % 2:k % 2 + 1], vare[:, k % 2:k % 2 + 1], ACT.Sqrt).then_inc(f_std, 1)

                def rows(nb, outputs):
                    if outputs is not None:
                        for k in range(TC):
                            root(outputs, k)
                        act.wait_ge(f_mm, TC * (outputs + 1))
                    for d in range(KD):
                        act.wait_ge(g_mm, KD * nb + d + 1)
                        nc.scalar.activation(G[:, HI, d, :], ps[:, BG + d, :], ACT.Copy).then_inc(g_hi, 1)

                rows(0, None)
                with act.Fori(1, NB) as nb:
                    rows(nb, nb - 1)
                for k in range(TC):
                    root(NB - 1, k)

            @block.vector
            def _(dve):
                nc.vector.tensor_scalar(std[:, :, :], stats[:, :, 1:2], EPS_LN, None, ALU.add).then_inc(n_var, 1)
                dve.wait_ge(n_std, 1)
                nc.vector.reciprocal(rstd[:, :, :], std[:, :, :]).then_inc(n_rstd, 1)
                dve.wait_ge(n_rstd, 1)
                with dve.Fori(0, NB // 2) as i:
                    for b in range(2):
                        dve.wait_ge(zg_in[b], 16 * (i + 1))
                        for k in range(TC):
                            n = TC * (2 * i + b) + k
                            nc.vector.tensor_scalar(z_in[:, b, k, :], z_in[:, b, k, :], stats[:, bass.ds(n, 1), 0],
                                                    rstd[:, bass.ds(n, 1), 0], ALU.subtract, ALU.mult)\
                                     .then_inc(x1_full, 1)
                        for k in range(TC):
                            n = TC * (2 * i + b) + k
                            dve.wait_ge(x1_hi, n + 1)
                            nc.vector.tensor_tensor(X1[:, LO, bass.ds(n, 1), :].rearrange("p a d -> p (a d)"),
                                                    z_in[:, b, k, :],
                                                    X1[:, HI, bass.ds(n, 1), :].rearrange("p a d -> p (a d)"),
                                                    ALU.subtract).then_inc(x1_lo, 1)

                for e in range(KD):
                    dve.wait_ge(w_hi, e + 1)
                    nc.vector.tensor_tensor(WT[:, LO, e, :], ps[:, 4 + e, :], WT[:, HI, e, :].bitcast(fp32),
                                            ALU.subtract).then_inc(w_lo, 1)

                def normalised(nb, k):
                    t = TC * nb + k
                    b = k % 2
                    dve.wait_ge(zf_in[b], 16 * (2 * nb + k // 2 + 1))
                    nc.vector.tensor_scalar(zf[:, b, :], zf[:, b, :], stats[:, bass.ds(t, 1), 0],
                                            rstd[:, bass.ds(t, 1), 0], ALU.subtract, ALU.mult).then_inc(f_x1, 1)

                def second_layer(nb, k):
                    t = TC * nb + k
                    b = k % 2
                    dve.wait_ge(f_mm, t + 1)
                    nc.vector.tensor_tensor(y[:, b, :], ps[:, BF + b, :], b1_rep[:, :], ALU.add).then_inc(f_out, 1)
                    dve.wait_ge(f_x1, t + 1)
                    dve.wait_ge(f_out, t + 1)
                    nc.vector.scalar_tensor_tensor(out=y[:, b, :], in0=y[:, b, :], scalar=0.0, in1=zf[:, b, :],
                                                   op0=ALU.max, op1=ALU.add).then_inc(f_sum, 1)
                    dve.wait_ge(f_sum, t + 1)
                    nc.vector.bn_stats(bst2[:, b, :], y[:, b, :]).then_inc(f_bn, 1)
                    dve.wait_ge(f_bn, t + 1)

                def variance(nb, k):
                    t = TC * nb + k
                    b = k % 2
                    nc.vector.bn_aggr(mv2[:, b, :], bst2[:, b, :]).then_inc(f_mv, 1)
                    dve.wait_ge(f_mv, t + 1)
                    nc.vector.tensor_scalar(vare[:, b:b + 1], mv2[:, b, 1:2], EPS_LN, None, ALU.add).then_inc(f_var, 1)

                def result(nb, k):
                    t = TC * nb + k
                    b = k % 2
                    dve.wait_ge(f_std, t + 1)
                    nc.vector.reciprocal(rstd2[:, b:b + 1], std2[:, b:b + 1]).then_inc(f_rstd, 1)
                    dve.wait_ge(f_rstd, t + 1)
                    wait(dve, out_st[b], 16 * (2 * nb + k // 2))
                    nc.vector.tensor_scalar(res[:, b, :], y[:, b, :], mv2[:, b, 0:1], rstd2[:, b:b + 1],
                                            ALU.subtract, ALU.mult).then_inc(f_res, 1)

                def outputs(nb):
                    normalised(nb, 0)
                    second_layer(nb, 0)
                    normalised(nb, 1)
                    variance(nb, 0)
                    for k in range(1, TC):
                        second_layer(nb, k)
                        result(nb, k - 1)
                        variance(nb, k)
                        if k + 1 < TC:
                            normalised(nb, k + 1)
                    result(nb, TC - 1)

                def g_split(nb):
                    for d in range(KD):
                        dve.wait_ge(g_hi, KD * nb + d + 1)
                        nc.vector.tensor_tensor(G[:, LO, d, :], ps[:, BG + d, :], G[:, HI, d, :].bitcast(fp32),
                                                ALU.subtract).then_inc(g_lo, 1)

                dve.wait_ge(b1_in, 16)
                g_split(0)
                outputs(0)
                g_split(1)
                with dve.Fori(2, NB) as nb:
                    outputs(nb - 1)
                    g_split(nb)
                outputs(NB - 1)

            @block.gpsimd
            def _(pool):
                def z_load(t, b):
                    pool.dma_start(zf[:, b, :], z_dram[bass.ds(t * P, P), :]).then_inc(zf_in[b], 16)

                def store(t, b):
                    pool.wait_ge(f_res, t + 1)
                    pool.dma_start(out[bass.ds(t * P, P), :], res[:, b, :]).then_inc(out_st[b], 16)

                for b in range(2):
                    z_load(b, b)
                with pool.Fori(0, NT // 2 - 1) as i:
                    for b in range(2):
                        store(2 * i + b, b)
                        z_load(2 * i + 2 + b, b)
                for b in range(2):
                    store(NT - 2 + b, b)
                for b in range(2):
                    pool.wait_ge(out_st[b], 16 * (NT // 2))

        work.close()


_INS = ["x", "adj", "L0_gnn_key", "L0_gnn_value", "L0_gnn_Wq", "L0_gnn_bq", "L0_gnn_Wk", "L0_gnn_bk", "L0_gnn_Wv",
        "L0_gnn_bv", "L0_gnn_Wm", "L0_gnn_bm", "L1_gnn_W", "L1_gnn_b"]


def kernel(**inputs):
    import numpy as _np
    import concourse.bacc as _bacc
    from concourse.bass_utils import run_bass_kernel_spmd as _run

    nc = _bacc.Bacc("TRN2", target_bir_lowering=False, num_devices=1)
    arrays, args = {}, []
    for name in _INS:
        a = _np.ascontiguousarray(inputs[name])
        arrays["in_" + name] = a
        args.append(nc.dram_tensor("in_" + name, a.shape, mybir.dt.from_np(a.dtype), kind="ExternalInput").ap())
    args.append(nc.dram_tensor("out_0", (4096, 512), fp32, kind="ExternalOutput").ap())
    attention_then_aggregation(nc, *args)
    r = _run(nc, [arrays], core_ids=[0])
    return r.results[0]["out_0"]
```

```python
import concourse.bass as bass
from concourse import mybir
from contextlib import ExitStack

fp32 = mybir.dt.float32
f32r = mybir.dt.float32r
fp16 = mybir.dt.float16
bf16 = mybir.dt.bfloat16
ALU = mybir.AluOpType
ACT = mybir.ActivationFunctionType
AX = mybir.AxisListType

HI, LO = 0, 1
PASSES = ((HI, HI), (LO, HI), (HI, LO))


def wait(eng, sem, value):
    if not isinstance(value, int) or value > 0:
        eng.wait_ge(sem, value)


def attention_then_aggregation(nc, x, adj, key, value, wq, bq, wk, bk, wv, bv, wm, bm, w1, b1, out):
    N, D = x.shape
    P = 128
    KD = D // P
    NT = N // P
    HALF = N // 2
    MT = HALF // P
    C = 512
    MC = HALF // C
    TC = C // P
    SCALE = 1.0 / float(N) ** 0.5
    EPS_SCORE = 1e-5
    MASKED = -1e9
    EPS_LN = 1e-5

    ctx = ExitStack()

    def sb(scope, name, shape, dt):
        return scope.enter_context(nc.sbuf_tensor(name, shape, dt))

    def sem(name):
        return ctx.enter_context(nc.semaphore(name))

    t_dram = nc.dram_tensor("t_dram", [NT, P, 2 * D], fp32).ap()
    kt_dram = nc.dram_tensor("kt_dram", [P, 2, KD, HALF], fp32).ap()
    vp_dram = nc.dram_tensor("vp_dram", [P, 2, MT, D], fp32).ap()
    o_dram = nc.dram_tensor("o_dram", [N, D], fp32).ap()
    adj_bf = nc.dram_tensor("adj_bf", [N, N], bf16).ap()
    z_dram = nc.dram_tensor("z_dram", [N, D], fp32).ap()

    with ctx:
        ps = ctx.enter_context(nc.psum_tensor("ps", [P, 8, C], fp32))
        ident = sb(ctx, "ident", [P, P], fp32)
        c_all = sb(ctx, "c_all", [P, NT], fp32)
        bias_o = sb(ctx, "bias_o", [P, D], fp32)
        neg_max = sb(ctx, "neg_max", [P, NT, 2], fp32)
        row_sum = sb(ctx, "row_sum", [P, NT, 2], fp32)
        stats = sb(ctx, "stats", [P, NT, 2], fp32)

        std = sb(ctx, "std", [P, NT, 1], fp32)
        rstd = sb(ctx, "rstd", [P, NT, 1], fp32)
        bst2 = sb(ctx, "bst2", [P, TC, 6], fp32)
        mv2 = sb(ctx, "mv2", [P, TC, 2], fp32)
        vare = sb(ctx, "vare", [P, TC], fp32)
        std2 = sb(ctx, "std2", [P, TC], fp32)
        rstd2 = sb(ctx, "rstd2", [P, TC], fp32)

        resident = ctx.enter_context(ExitStack())
        with ExitStack() as split:
            wq_s = sb(split, "wq_s", [P, 2, KD, D], f32r)
            wk_s = sb(split, "wk_s", [P, 2, KD, D], f32r)
            wv_s = sb(split, "wv_s", [P, 2, KD, D], f32r)
            wmT_s = sb(split, "wmT_s", [P, 2, KD, D], f32r)
        KT = sb(resident, "KT", [P, 2, KD, HALF], f32r)
        with ExitStack() as raw:
            wa = sb(raw, "wa", [P, KD, D], fp32)
            wb = sb(raw, "wb", [P, KD, D], fp32)
            wd = sb(raw, "wd", [P, KD, D], fp32)
            wc = sb(raw, "wc", [P, KD, D], fp32)
        VP = sb(resident, "VP", [P, 2, MT, D], f32r)
        prep = resident.enter_context(ExitStack())
        Aq = sb(prep, "Aq", [P, 2, KD, D], f32r)
        Wvm = sb(prep, "Wvm", [P, 2, KD, D], f32r)
        bq_k = sb(prep, "bq_k", [P, KD, 1], fp32)
        bk_q = sb(prep, "bk_q", [P, D], fp32)
        bqbk = sb(prep, "bqbk", [P, 1], fp32)

        bcol = sb(prep, "bcol", [P, 3, KD], fp32)
        brep = sb(prep, "brep", [P, 2, 3, KD, P], f32r)
        bb = sb(prep, "bb", [P, KD], fp32)
        ones = sb(prep, "ones", [P, P], fp32)
        s_ident, s_one = sem("ident_made"), sem("ones_made")
        s_w = [sem("wq_wk_in%d" % e) for e in range(KD)]
        s_wv, s_wm, s_bc, s_bm = sem("wv_in"), sem("wm_in"), sem("bias_columns_in"), sem("bm_in")
        s_rhi, s_rep, s_bb = sem("bias_repeated_hi"), sem("bias_repeated"), sem("bq_bk_multiplied")
        s_whi, s_wlo = sem("raw_weights_hi"), sem("raw_weights_split")
        s_mhi, s_bsum = sem("wm_hi"), sem("bqbk_out")
        s_amm, s_ahi, s_alo = sem("aq_made"), sem("aq_hi"), sem("aq_lo")
        s_rmm, s_rout, s_bqt = sem("bias_rows_made"), sem("bias_rows_out"), sem("bq_k_transposed")
        s_wmt, s_wmc = sem("wm_transposed"), sem("wm_lo")
        s_vmm, s_vhi, s_vlo = sem("wvm_made"), sem("wvm_hi"), sem("wvm_lo")
        s_bmm, s_bout = sem("bias_o_made"), sem("bias_o_out")

        work = ExitStack()
        rows = sb(work, "rows", [P, 4, D], fp32)
        valueT = sb(work, "valueT", [P, 2, 2, D], f32r)
        c_tmp = sb(work, "c_tmp", [P, 2], fp32)
        xu = sb(work, "xu", [P, D], fp32)
        row_in = [sem("row_in%d" % j) for j in range(4)]
        x_tr, xt_hi, xt_lo = sem("x_tr"), sem("xt_hi"), sem("xt_lo")
        c_sum, c_out = sem("c_sum"), sem("c_out")
        t_mm, t_hi, t_lo = sem("t_mm"), sem("t_hi"), sem("t_lo")
        t_st = [sem("t_st%d" % b) for b in range(2)]
        k_tr, k_hi, k_lo = sem("k_tr"), sem("k_hi"), sem("k_lo")
        v_tr, vt_hi, vt_lo = sem("v_tr"), sem("vt_hi"), sem("vt_lo")
        v_mm, vp_hi, vp_lo = sem("v_mm"), sem("vp_hi"), sem("vp_lo")
        kt_st, vp_st = sem("kt_st"), sem("vp_st")
        BA, BB, BC = 0, 2, 4
        NG = N // C

        def xT(slot, s):
            return VP[:, s, slot * KD:(slot + 1) * KD, :]

        def queries(slot, s):
            return VP[:, s, 2 * KD + slot * TC:2 * KD + (slot + 1) * TC, :]

        def transposes(bank, slot):
            for k in range(KD):
                last = nc.tensor.transpose(ps[:, bank, k * P:(k + 1) * P], rows[:, slot, k * P:(k + 1) * P], ident[:, :])
            return last

        def group_loop(eng, group):
            for b in range(2):
                group(b, b, True)
            with eng.Fori(1, NG // 2 - 1) as i:
                for b in range(2):
                    group(2 * i + b, b, True)
            for b in range(2):
                group(NG - 2 + b, b, b == 0)

        work.close()
        prep.close()

        work = ExitStack()
        adj_rows = sb(work, "adj_rows", [P, 2, HALF], fp32)
        prob = sb(work, "prob", [P, 2, HALF], fp32)
        small = sb(work, "small", [P, 2, C], fp32)
        t_in = sb(work, "t_in", [P, 2, 2, D], f32r)
        probT = sb(work, "probT", [P, 2, 2, C], f32r)
        x_in = sb(work, "x_in", [P, 2, D], fp32)
        o_in = sb(work, "o_in", [P, 2, D], fp32)
        z_out = sb(work, "z_out", [P, 2, D], fp32)
        chunk_max = sb(work, "chunk_max", [P, 2, MC], fp32)
        nmax = sb(work, "nmax", [P, 2], fp32)
        rsum = sb(work, "rsum", [P, 2], fp32)
        c_now = sb(work, "c_now", [P, 2], fp32)
        nm_pair = sb(work, "nm_pair", [P, 2, 2], fp32)
        ls_pair = sb(work, "ls_pair", [P, 2, 2], fp32)
        nm = sb(work, "nm", [P, 2], fp32)
        wgt = sb(work, "wgt", [P, 2, 2], fp32)
        wls = sb(work, "wls", [P, 2, 2], fp32)
        den = sb(work, "den", [P, 2], fp32)
        rden = sb(work, "rden", [P, 2], fp32)
        wn = sb(work, "wn", [P, 2, 2], fp32)
        bst = sb(work, "bst", [P, 2, 6], fp32)
        mv = sb(work, "mv", [P, 2, 2], fp32)
        adj_in = [sem("adj_in%d" % b) for b in range(2)]
        q_in = [sem("queries_in%d" % b) for b in range(2)]
        xo_in = [sem("x_and_o_in%d" % b) for b in range(2)]
        kt_in = [sem("kt_in%d" % c) for c in range(MC)]
        vp_in = [sem("vp_in%d" % c) for c in range(MC)]
        s_mm, s_adj = sem("scores_made"), sem("scores_masked")
        s_abs, s_neg = sem("magnitude_made"), sem("threshold_made")
        s_mask = sem("threshold_added")
        s_max, s_exp, s_keep = sem("row_maximum"), sem("exponentials_made"), sem("row_sum_kept")
        s_c = sem("c_copied")
        p_tr, p_hi, p_lo = sem("prob_transposed"), sem("probT_hi"), sem("probT_lo")
        p_use = sem("probT_used")
        o_mm = sem("output_made")
        ab_st = [sem("adj_stored%d" % b) for b in range(2)]
        o_out = sem("output_out")
        o_st = [sem("output_stored%d" % b) for b in range(2)]
        m_step, m_w = sem("merge_step"), sem("merge_maximum_and_weights")
        xb, s_mv = sem("bias_added"), sem("mean_and_variance")
        BS, BP, BO = 0, 4, 6
        work.close()
        resident.close()

        QUARTER = N // 4
        QT = QUARTER // P
        second = ExitStack()
        X1 = sb(second, "X1", [P, 2, NT, D], fp16)
        WT = sb(second, "WT", [P, 2, KD, D], f32r)
        G = sb(second, "G", [P, 2, KD, C], f32r)
        w_raw = sb(second, "w_raw", [P, KD, D], fp32)
        zf = sb(second, "zf", [P, TC, D], fp32)
        y = sb(second, "y", [P, TC, D], fp32)
        res = sb(second, "res", [P, TC, D], fp32)
        z_in = sb(second, "z_in", [P, 2, TC, D], fp32)
        adjT = sb(second, "adjT", [P, 4, QT, C], bf16)
        b1_rep = sb(second, "b1_rep", [P, D], fp32)
        second.close()
        w_in, b1_in = sem("w1_in"), sem("b1_in")
        s_stat = sem("stats_kept")
        n_var, n_std, n_rstd = sem("variances"), sem("deviations"), sem("inverse_deviations")
        zg_in = [sem("z_group_in%d" % b) for b in range(2)]
        x1_full, x1_hi, x1_lo = sem("x1_normalised"), sem("x1_hi"), sem("x1_lo")
        w_tr, w_hi, w_lo = sem("w1_transposed"), sem("w1_hi"), sem("w1_lo")
        aq_in = [sem("adj_quarter_in%d" % q) for q in range(4)]
        a_use = sem("adj_quarter_used")
        g_mm, g_hi, g_lo = sem("aggregate_made"), sem("aggregate_hi"), sem("aggregate_lo")
        f_mm, f_out = sem("second_product_made"), sem("second_product_out")
        zf_in = [sem("z_tile_in%d" % k) for k in range(TC)]
        f_x1, f_sum, f_bn = sem("residual_made"), sem("residual_added"), sem("output_bn_stats")
        f_mv, f_var, f_std = sem("output_mean_variance"), sem("output_variance"), sem("output_deviation")
        f_rstd, f_res = sem("output_inverse_deviation"), sem("result_made")
        out_st = [sem("result_stored%d" % k) for k in range(TC)]
        last_st = sem("last_results_stored")
        BG, BF = 0, 6
        NB = N // C
        FIRST_F, NEXT_F = 2, 3

        with nc.Block() as block:

            @block.sync
            def _(sp):
                for e in range(KD):
                    sp.dma_start(wa[:, e, :], wq[e * P:(e + 1) * P, :]).then_inc(s_w[e], 16)
                    sp.dma_start(wb[:, e, :], wk[e * P:(e + 1) * P, :]).then_inc(s_w[e], 16)
                with nc.allow_non_contiguous_dma(reason="three bias vectors, once"):
                    for n, b in enumerate((bq, bk, bv)):
                        sp.dma_start(bcol[:, n, :], b.rearrange("(k p) -> p k", p=P)).then_inc(s_bc, 16)
                sp.dma_start(bias_o[:, :], bm.rearrange("(a n) -> a n", a=1).to_broadcast([P, D])).then_inc(s_bm, 16)
                sp.dma_start(wc[:, :, :], wv.rearrange("(e p) d -> p e d", p=P)).then_inc(s_wv, 16)
                sp.dma_start(wd[:, :, :], wm.rearrange("(o p) e -> p o e", p=P)).then_inc(s_wm, 16)

                def x_loads(G):
                    for j in range(TC):
                        n = TC * G + j
                        wait(sp, x_tr, n - TC + 1)
                        wait(sp, c_sum, n - TC + 1)
                        sp.dma_start(rows[:, j, :], x[bass.ds(n * P, P), :]).then_inc(row_in[j], 16)

                def kv_loads(i, section):
                    half = (1 - section) * HALF
                    for b in range(2):
                        g = section * MT + 2 * i + b
                        wait(sp, k_tr, g - 1)
                        sp.dma_start(rows[:, b, :], key[bass.ds(half + (2 * i + b) * P, P), :]).then_inc(row_in[b], 16)
                        wait(sp, v_tr, g - 1)
                        sp.dma_start(rows[:, 2 + b, :], value[bass.ds(half + (2 * i + b) * P, P), :])\
                          .then_inc(row_in[2 + b], 16)

                x_loads(0)
                with sp.Fori(1, NG) as G:
                    x_loads(G)
                sp.wait_ge(x_tr, NT)
                sp.wait_ge(c_sum, NT)
                for section in range(2):
                    kv_loads(0, section)
                    with sp.Fori(1, MT // 2) as i:
                        kv_loads(i, section)

                def load_queries(g, n, b):
                    wait(sp, s_mm, MC * (g - 1))
                    sp.dma_start(t_in[:, b, :, :].rearrange("p s d -> p (s d)").bitcast(fp32), t_dram[n, :, :])\
                      .then_inc(q_in[b], 16)

                def load_adjacency(g, n, b, half):
                    if not isinstance(g, int) or g >= 2:
                        sp.wait_ge(ab_st[b], 8 * (g - b))
                    sp.dma_start(adj_rows[:, b, :], adj[bass.ds(n * P, P), half * HALF:(half + 1) * HALF])\
                      .then_inc(adj_in[b], 16)

                def loads(g, n, b, half):
                    load_queries(g, n, b)
                    load_adjacency(g, n, b, half)

                def loads_x_o(n, b):
                    sp.dma_start(x_in[:, b, :], x[bass.ds(n * P, P), :]).then_inc(xo_in[b], 16)
                    sp.dma_start(o_in[:, b, :], o_dram[bass.ds(n * P, P), :]).then_inc(xo_in[b], 16)

                def store(g, n, b, half):
                    sp.wait_ge(o_out, g + 1)
                    dst = z_dram if half == 1 else o_dram
                    sp.dma_start(dst[bass.ds(n * P, P), :], z_out[:, b, :]).then_inc(o_st[b], 16)

                for b in range(2):
                    sp.wait_ge(t_st[b], 8 * TC * NG)
                for n in range(3):
                    loads(n, n, n % 2, 0)
                with sp.Fori(1, NT // 2 - 1) as i:
                    for b in range(2):
                        loads(2 * i + b + 1, 2 * i + b + 1, 1 - b, 0)
                        store(2 * i + b - 2, 2 * i + b - 2, b, 0)
                loads(NT - 1, NT - 1, 1, 0)
                for n in (NT - 4, NT - 3):
                    store(n, n, n % 2, 0)
                sp.wait_ge(kt_st, 16 * 2 * KD * MC)
                sp.wait_ge(vp_st, 16 * MT)
                for c in range(MC):
                    sp.wait_ge(s_mm, MC * (NT - 1) + c + 1)
                    sp.dma_start(KT[:, :, :, c * C:(c + 1) * C].rearrange("p s k n -> p (s k) n").bitcast(fp32),
                                 kt_dram[:, :, :, c * C:(c + 1) * C].rearrange("p s k n -> p (s k) n"))\
                      .then_inc(kt_in[c], 16)
                loads(NT, 0, 0, 1)
                store(NT - 2, NT - 2, 0, 0)
                loads(NT + 1, 1, 1, 1)
                for c in range(MC):
                    if c < MC - 1:
                        sp.wait_ge(p_use, (MC - 1) * (NT - 1) + c + 1)
                    else:
                        sp.wait_ge(o_mm, NT)
                    if c == 3:
                        load_queries(NT + 2, 2, 0)
                    sp.dma_start(VP[:, :, c * TC:(c + 1) * TC, :].bitcast(fp32),
                                 vp_dram[:, :, c * TC:(c + 1) * TC, :]).then_inc(vp_in[c], 16)
                load_adjacency(NT + 2, 2, 0, 1)
                store(NT - 1, NT - 1, 1, 0)
                for b in range(2):
                    sp.wait_ge(o_st[b], 16 * (NT // 2))
                for b in range(2):
                    loads_x_o(b, b)
                with sp.Fori(1, NT // 2 - 1) as i:
                    for b in range(2):
                        loads(NT + 2 * i + b + 1, 2 * i + b + 1, 1 - b, 1)
                        store(NT + 2 * i + b - 2, 2 * i + b - 2, b, 1)
                        loads_x_o(2 * i + b, b)
                loads(2 * NT - 1, NT - 1, 1, 1)
                for n in (NT - 4, NT - 3):
                    store(NT + n, n, n % 2, 1)
                    loads_x_o(n + 2, n % 2)

                def z_group(g):
                    wait(sp, x1_lo, TC * (g - 1))
                    sp.dma_start(z_in[:, g % 2, :, :],
                                 z_dram[g * C:(g + 1) * C, :].rearrange("(k p) d -> p k d", p=P)).then_inc(zg_in[g % 2], 16)

                def adj_quarter(nb, q):
                    sp.dma_start_transpose(adjT[:, q, :, :], adj_bf[bass.ds(nb * C, C), q * QUARTER:(q + 1) * QUARTER])\
                      .then_inc(aq_in[q], 16)

                for b in range(2):
                    sp.wait_ge(o_st[b], 16 * (NT - 2))
                    sp.wait_ge(ab_st[b], 16 * NT)
                z_group(0)
                sp.wait_ge(p_tr, MC * (2 * NT - 1))
                adj_quarter(0, 0)
                z_group(1)
                sp.wait_ge(p_tr, MC * 2 * NT)
                adj_quarter(0, 1)
                z_group(2)
                sp.wait_ge(o_mm, 2 * NT)
                sp.wait_ge(s_mask, MC * 2 * NT)
                adj_quarter(0, 2)
                z_group(3)
                sp.dma_start(w_raw[:, :, :], w1.rearrange("(o p) e -> p o e", p=P)).then_inc(w_in, 16)
                sp.dma_start(b1_rep[:, :], b1.rearrange("(a n) -> a n", a=1).to_broadcast([P, D])).then_inc(b1_in, 16)
                store(2 * NT - 2, NT - 2, 0, 1)
                z_group(4)
                adj_quarter(0, 3)
                z_group(5)
                store(2 * NT - 1, NT - 1, 1, 1)
                z_group(6)
                for b in range(2):
                    sp.wait_ge(o_st[b], 16 * NT)
                z_group(7)
                with sp.Fori(1, NB) as nb:
                    for q in range(4):
                        if q < 3:
                            sp.wait_ge(a_use, 3 * (nb - 1) + q + 1)
                        else:
                            sp.wait_ge(g_mm, KD * nb)
                        adj_quarter(nb, q)
                for k in range(TC):
                    t = NT - TC + k
                    sp.wait_ge(f_res, t + 1)
                    sp.dma_start(out[t * P:(t + 1) * P, :], res[:, k, :]).then_inc(last_st, 16)
                sp.wait_ge(last_st, 16 * TC)
                for k in range(TC):
                    sp.wait_ge(out_st[k], 16 * (NB - 1))

            @block.gpsimd
            def _(pool):
                nc.gpsimd.memset(ident[:, :], 0.0).then_inc(s_ident, 1)
                nc.gpsimd.memset(ones[:, :], 1.0).then_inc(s_one, 1)
                pool.wait_ge(s_ident, 1)
                nc.gpsimd.affine_select(out=ident[:, :], in_=ident[:, :], compare_op=ALU.not_equal, fill=1.0,
                                        base=0, pattern=[[-1, P]], channel_multiplier=1).then_inc(s_ident, 1)

                with pool.Fori(0, NG // 2) as i:
                    for b in range(2):
                        G = 2 * i + b
                        pool.wait_ge(t_lo, KD * (G + 1))
                        for j in range(TC):
                            tile = 2 * KD + b * TC + j
                            pool.dma_start(t_dram[bass.ds(TC * G + j, 1), :, :].rearrange("a p (s d) -> p s (a d)", s=2),
                                           VP[:, :, tile, :].bitcast(fp32)).then_inc(t_st[b], 16)
                for c in range(MC):
                    wait(pool, kt_st, 16 * 2 * KD * c)
                    wait(pool, vp_st, 16 * TC * c)
                    pool.wait_ge(k_lo, TC * (c + 1))
                    for s in (HI, LO):
                        for k in range(KD):
                            pool.dma_start(kt_dram[:, s, k, c * C:(c + 1) * C],
                                           KT[:, s, k, c * C:(c + 1) * C].bitcast(fp32)).then_inc(kt_st, 16)
                    pool.wait_ge(vp_lo, TC * (c + 1))
                    for m in range(c * TC, (c + 1) * TC):
                        pool.dma_start(vp_dram[:, :, m, :], VP[:, :, m, :].bitcast(fp32)).then_inc(vp_st, 16)

                for half in range(2):
                    with pool.Fori(0, NT // 2) as i:
                        for b in range(2):
                            pool.wait_ge(s_adj, MC * (half * NT + 2 * i + b + 1))
                            pool.dma_start(adj_bf[bass.ds((2 * i + b) * P, P), half * HALF:(half + 1) * HALF],
                                           adj_rows[:, b, :]).then_inc(ab_st[b], 16)

                def z_load(t, k):
                    pool.dma_start(zf[:, k, :], z_dram[bass.ds(t * P, P), :]).then_inc(zf_in[k], 16)

                def store(t, k):
                    pool.wait_ge(f_res, t + 1)
                    pool.dma_start(out[bass.ds(t * P, P), :], res[:, k, :]).then_inc(out_st[k], 16)

                pool.wait_ge(x1_lo, NT)
                for k in range(TC):
                    z_load(k, k)
                with pool.Fori(0, NB - 1) as nb:
                    for k in range(TC):
                        store(TC * nb + k, k)
                        z_load(TC * nb + k + TC, k)

            @block.tensor
            def _(pe):
                def bias_row(bank, b, w):
                    for e in range(KD):
                        for q, (u, v) in enumerate(PASSES):
                            last = nc.tensor.matmul(ps[:, bank, :], brep[:, u, b, e, :], w[:, v, e, :],
                                                    start=(e == 0 and q == 0), stop=(e == KD - 1 and q == 2))
                    return last

                def x_turn(G, j):
                    n = TC * G + j
                    pe.wait_ge(row_in[j], 16 * (G + 1))
                    wait(pe, xt_lo, n - 1)
                    transposes(BA + j % 2, j).then_inc(x_tr, 1)

                for e in range(KD):
                    pe.wait_ge(s_wlo, 2 * (e + 1))
                    for d in range(KD):
                        for q, (u, w) in enumerate(PASSES):
                            last = nc.tensor.matmul(ps[:, d, :], wq_s[:, u, e, d * P:(d + 1) * P], wk_s[:, w, e, :],
                                                    start=(e == 0 and q == 0), stop=(e == KD - 1 and q == 2))
                        if e == KD - 1:
                            last.then_inc(s_amm, 1)
                pe.wait_ge(s_rep, 3)
                bias_row(4, 0, wk_s).then_inc(s_rmm, 1)
                bias_row(5, 1, wq_s).then_inc(s_rmm, 1)
                pe.wait_ge(s_bb, 1)
                nc.tensor.matmul(ps[:, 6, 0:KD], ones[:, :], bb[:, :], start=True, stop=True).then_inc(s_rmm, 1)
                pe.wait_ge(s_wm, 16)
                pe.wait_ge(s_ident, 2)
                pe.wait_ge(s_alo, KD)
                for e in range(KD):
                    for o in range(KD):
                        last = nc.tensor.transpose(ps[:, e, o * P:(o + 1) * P], wd[:, o, e * P:(e + 1) * P], ident[:, :])
                    last.then_inc(s_wmt, 1)
                pe.wait_ge(s_rout, 3)
                for k in range(KD):
                    last = nc.tensor.transpose(ps[:, 7, k * P:(k + 1) * P], xu[:, k * P:(k + 1) * P], ident[:, :])
                last.then_inc(s_bqt, 1)
                pe.wait_ge(s_wmc, 2)
                for j in range(2):
                    x_turn(0, j)
                pe.wait_ge(s_wmc, KD)
                pe.wait_ge(s_wlo, 3 * KD)
                pe.wait_ge(s_rout, 4)
                for d in range(KD):
                    for e in range(KD):
                        for q, (u, w) in enumerate(PASSES):
                            last = nc.tensor.matmul(ps[:, 4 + d, :], wv_s[:, u, e, d * P:(d + 1) * P], wmT_s[:, w, e, :],
                                                    start=(e == 0 and q == 0), stop=(e == KD - 1 and q == 2))
                    last.then_inc(s_vmm, 1)
                    if d < 2:
                        x_turn(0, 2 + d)
                bias_row(3, 2, wmT_s).then_inc(s_bmm, 1)

                def query_features(G, b, e):
                    pe.wait_ge(xt_lo, TC * (G + 1))
                    wait(pe, t_lo, KD * (G - 1) + e + 1)
                    n = 0
                    for s, m in PASSES:
                        for k in range(KD):
                            last = nc.tensor.matmul(ps[:, BC + e, :], Aq[:, m, k, e * P:(e + 1) * P], xT(b, s)[:, k, :],
                                                    start=(n == 0), stop=(n == 3 * KD - 1))
                            n += 1
                    last.then_inc(t_mm, 1)

                def group(G, b, turn_next):
                    for e in range(KD):
                        if turn_next:
                            x_turn(G + 1, e)
                        query_features(G, b, e)

                def value_project(g, b):
                    pe.wait_ge(vt_lo, g + 1)
                    wait(pe, vp_lo, g - 1)
                    n = 0
                    for s, m in PASSES:
                        for k in range(KD):
                            last = nc.tensor.matmul(ps[:, BC + b, :], valueT[:, b, s, k * P:(k + 1) * P], Wvm[:, m, k, :],
                                                    start=(n == 0), stop=(n == 3 * KD - 1))
                            n += 1
                    last.then_inc(v_mm, 1)

                def kv_chunk(section, c):
                    for j in range(TC):
                        b = j % 2
                        g = section * MT + TC * c + j
                        pair = section * MT // 2 + TC // 2 * c + j // 2 + 1
                        pe.wait_ge(row_in[b], 16 * (NG + pair))
                        wait(pe, k_lo, g - 1)
                        transposes(BA + b, b).then_inc(k_tr, 1)
                        pe.wait_ge(row_in[2 + b], 16 * (NG + pair))
                        wait(pe, vt_lo, g - 1)
                        transposes(BB + b, 2 + b).then_inc(v_tr, 1)
                        if not (isinstance(g, int) and g == 0):
                            value_project(g - 1, 1 - b)

                pe.wait_ge(s_vlo, KD)
                group_loop(pe, group)
                pe.wait_ge(xt_lo, NT)
                pe.wait_ge(t_lo, KD * NG - 2)
                for section in range(2):
                    kv_chunk(section, 0)
                    with pe.Fori(1, MC) as c:
                        kv_chunk(section, c)
                value_project(NT - 1, 1)

                def scores(g, b, c):
                    wait(pe, s_adj, MC * (g - 1) + c + 1)
                    n = 0
                    for s, m in PASSES:
                        for k in range(KD):
                            last = nc.tensor.matmul(ps[:, BS + c, :], t_in[:, b, s, k * P:(k + 1) * P],
                                                    KT[:, m, k, c * C:(c + 1) * C],
                                                    start=(n == 0), stop=(n == 3 * KD - 1))
                            n += 1
                    last.then_inc(s_mm, 1)

                def turn(g, b, r):
                    if isinstance(g, int) and g == 0 and r == 0:
                        pe.wait_ge(vp_lo, NT)
                    if r == 0:
                        pe.wait_ge(s_exp, g + 1)
                    wait(pe, p_lo, MC * g + r - 1)
                    for j in range(TC):
                        m = r * TC + j
                        last = nc.tensor.transpose(ps[:, BP + r % 2, j * P:(j + 1) * P],
                                                   prob[:, b, m * P:(m + 1) * P], ident[:, :])
                    last.then_inc(p_tr, 1)

                def weigh(g, b, r):
                    if r == 0:
                        wait(pe, o_out, g - 1)
                    pe.wait_ge(p_lo, MC * g + r + 1)
                    for j in range(TC):
                        m = r * TC + j
                        for q, (s, v) in enumerate(PASSES):
                            last = nc.tensor.matmul(ps[:, BO + b, :], probT[:, r % 2, s, j * P:(j + 1) * P], VP[:, v, m, :],
                                                    start=(m == 0 and q == 0), stop=(m == MT - 1 and q == 2))
                    last.then_inc(o_mm, 1) if r == MC - 1 else last.then_inc(p_use, 1)

                def step(g, b, i, half, make, use):
                    if make:
                        pe.wait_ge(q_in[b], 16 * (half * NT // 2 + i + 1))
                    for c in range(MC):
                        if make:
                            if half == 1 and not use:
                                pe.wait_ge(kt_in[c], 16)
                            scores(g, b, c)
                        if use and c in (1, 2):
                            turn(g - 1, 1 - b, c - 1)
                    if use:
                        for r in range(MC):
                            if half == 1 and isinstance(i, int) and i == 0:
                                pe.wait_ge(vp_in[r], 16)
                            weigh(g - 1, 1 - b, r)
                            if r + 2 < MC:
                                turn(g - 1, 1 - b, r + 2)

                pe.wait_ge(k_lo, NT)
                pe.wait_ge(vt_lo, NT)
                for half in range(2):
                    g0 = half * NT
                    step(g0, 0, 0, half, True, False)
                    step(g0 + 1, 1, 0, half, True, True)
                    for b in range(2):
                        step(g0 + 2 + b, b, 1, half, True, True)
                    with pe.Fori(2, NT // 2) as i:
                        for b in range(2):
                            step(g0 + 2 * i + b, b, i, half, True, True)
                    step(g0 + NT, 0, None, half, False, True)

                def second_weights():
                    pe.wait_ge(w_in, 16)
                    pe.wait_ge(o_out, 2 * NT)
                    for e in range(KD):
                        for o in range(KD):
                            last = nc.tensor.transpose(ps[:, 4 + e, o * P:(o + 1) * P], w_raw[:, o, e * P:(e + 1) * P],
                                                       ident[:, :])
                        last.then_inc(w_tr, 1)

                def aggregate(nb, m):
                    q = m // QT
                    if m % QT == 0:
                        pe.wait_ge(aq_in[q], 16 * (nb + 1))
                    for d in range(KD):
                        if m == 0:
                            wait(pe, g_lo, KD * (nb - 1) + d + 1)
                        for s in (HI, LO):
                            last = nc.tensor.matmul(ps[:, BG + d, :], X1[:, s, m, d * P:(d + 1) * P], adjT[:, q, m % QT, :],
                                                    start=(m == 0 and s == HI), stop=(m == NT - 1 and s == LO))
                        if m == NT - 1:
                            last.then_inc(g_mm, 1)
                    if m % QT == QT - 1 and m < NT - 1:
                        last.then_inc(a_use, 1)

                def output(nb, k):
                    wait(pe, f_out, TC * nb + max(k - 1, 0))
                    for d in range(KD):
                        if k == 0:
                            pe.wait_ge(g_lo, KD * nb + d + 1)
                        for q, (u, w) in enumerate(PASSES):
                            last = nc.tensor.matmul(ps[:, BF + k % 2, :], G[:, u, d, k * P:(k + 1) * P], WT[:, w, d, :],
                                                    start=(d == 0 and q == 0), stop=(d == KD - 1 and q == 2))
                    last.then_inc(f_mm, 1)

                def rows(nb, outputs):
                    for m in range(NT):
                        if outputs is None:
                            pe.wait_ge(x1_lo, m + 1)
                            if m == 2 * QT:
                                second_weights()
                        aggregate(nb, m)
                        if outputs is not None and m >= FIRST_F and (m - FIRST_F) % NEXT_F == 0 \
                                and (m - FIRST_F) // NEXT_F < TC:
                            output(outputs, (m - FIRST_F) // NEXT_F)

                rows(0, None)
                pe.wait_ge(w_lo, KD)
                rows(1, 0)
                with pe.Fori(2, NB) as nb:
                    rows(nb, nb - 1)
                for k in range(TC):
                    output(NB - 1, k)

            @block.scalar
            def _(act):
                def x_out(G, b, j):
                    act.wait_ge(x_tr, TC * G + j + 1)
                    wait(act, t_mm, KD * (G - 1))
                    nc.scalar.activation(xT(b, HI)[:, :, j * P:(j + 1) * P],
                                         ps[:, BA + j % 2, :].rearrange("p (k n) -> p k n", n=P),
                                         ACT.Copy).then_inc(xt_hi, 1)

                for e in range(KD):
                    act.wait_ge(s_w[e], 32)
                    nc.scalar.activation(wq_s[:, HI, e, :], wa[:, e, :], ACT.Copy).then_inc(s_whi, 1)
                    nc.scalar.activation(wk_s[:, HI, e, :], wb[:, e, :], ACT.Copy).then_inc(s_whi, 1)
                act.wait_ge(s_bc, 48)
                act.wait_ge(s_one, 1)
                for b in range(3):
                    for e in range(KD):
                        last = nc.scalar.activation(brep[:, HI, b, e, :], ones[:, :], ACT.Copy, scale=bcol[:, b, e:e + 1])
                    last.then_inc(s_rhi, 1)
                act.wait_ge(s_wv, 16)
                for e in range(KD):
                    nc.scalar.activation(wv_s[:, HI, e, :], wc[:, e, :], ACT.Copy).then_inc(s_whi, 1)
                for d in range(KD):
                    act.wait_ge(s_amm, d + 1)
                    nc.scalar.activation(Aq[:, HI, d, :], ps[:, d, :], ACT.Copy, scale=SCALE).then_inc(s_ahi, 1)
                for e in range(KD):
                    act.wait_ge(s_wmt, e + 1)
                    nc.scalar.activation(wmT_s[:, HI, e, :], ps[:, e, :], ACT.Copy).then_inc(s_mhi, 1)
                for j in range(2):
                    x_out(0, 0, j)
                for d in range(KD):
                    act.wait_ge(s_vmm, d + 1)
                    nc.scalar.activation(Wvm[:, HI, d, :], ps[:, 4 + d, :], ACT.Copy).then_inc(s_vhi, 1)
                    if d < 2:
                        x_out(0, 0, 2 + d)

                def group(G, b, turn_next):
                    for e in range(KD):
                        if turn_next:
                            x_out(G + 1, 1 - b, e)
                        act.wait_ge(t_mm, KD * G + e + 1)
                        if not isinstance(G, int) or G >= 2:
                            act.wait_ge(t_st[b], 8 * TC * (G - b))
                        nc.scalar.activation(queries(b, HI)[:, :, e * P:(e + 1) * P],
                                             ps[:, BC + e, :].rearrange("p (j n) -> p j n", n=P),
                                             ACT.Identity, bias=bq_k[:, e, :]).then_inc(t_hi, 1)

                def value_out(g, tile, b):
                    act.wait_ge(v_mm, g + 1)
                    nc.scalar.activation(VP[:, HI, tile, :], ps[:, BC + b, :], ACT.Copy).then_inc(vp_hi, 1)

                def kv_chunk(section, c):
                    if section == 1:
                        act.wait_ge(kt_st, 16 * 2 * KD * (c + 1))
                        act.wait_ge(vp_st, 16 * TC * (c + 1))
                    for j in range(TC):
                        b = j % 2
                        tile = TC * c + j
                        g = section * MT + tile
                        act.wait_ge(k_tr, g + 1)
                        nc.scalar.activation(KT[:, HI, :, bass.ts(tile, P)],
                                             ps[:, BA + b, :].rearrange("p (k n) -> p k n", n=P),
                                             ACT.Copy).then_inc(k_hi, 1)
                        act.wait_ge(v_tr, g + 1)
                        wait(act, v_mm, g - 1)
                        nc.scalar.activation(valueT[:, b, HI, :], ps[:, BB + b, :], ACT.Copy).then_inc(vt_hi, 1)
                        if not isinstance(tile, int) or tile > 0:
                            value_out(g - 1, tile - 1, 1 - b)
                        elif section == 1:
                            value_out(g - 1, MT - 1, 1 - b)

                group_loop(act, group)
                for section in range(2):
                    kv_chunk(section, 0)
                    if section == 0:
                        for b in range(2):
                            act.wait_ge(t_st[b], 8 * TC * NG)
                    with act.Fori(1, MC) as c:
                        kv_chunk(section, c)
                value_out(NT - 1, MT - 1, 1)

                def magnitude(g, b, c):
                    act.wait_ge(s_adj, MC * g + c + 1)
                    wait(act, s_mask, MC * g + c - 1)
                    nc.scalar.activation(small[:, c % 2, :], prob[:, b, c * C:(c + 1) * C], ACT.Abs).then_inc(s_abs, 1)

                def exponentials(g, b):
                    act.wait_ge(s_max, g + 1)
                    wait(act, s_keep, g - 1)
                    nc.scalar.activation(prob[:, b, :], prob[:, b, :], ACT.Exp, bias=nmax[:, b:b + 1],
                                         accum_out=rsum[:, b:b + 1]).then_inc(s_exp, 1)

                def turned(g, r):
                    act.wait_ge(p_tr, MC * g + r + 1)
                    slot_free(g, r)
                    nc.scalar.activation(probT[:, r % 2, HI, :], ps[:, BP + r % 2, :], ACT.Copy).then_inc(p_hi, 1)

                def slot_free(g, r):
                    if r >= 2:
                        act.wait_ge(p_use, (MC - 1) * g + r - 1)
                    elif r == 1:
                        wait(act, o_mm, g)
                    else:
                        wait(act, p_use, (MC - 1) * g)

                def step(g, b, half, make, use, merge):
                    for c in range(MC):
                        if make:
                            magnitude(g, b, c)
                        if use and c in (1, 2):
                            turned(g - 1, c - 1)
                        if merge and c == 1:
                            finish(g - 2, b, half)
                    if use:
                        turned(g - 1, 2)
                        turned(g - 1, 3)
                    if make:
                        exponentials(g, b)

                def finish(g, b, half):
                    if half == 0:
                        act.wait_ge(o_mm, g + 1)
                        if not isinstance(g, int) or g >= 2:
                            act.wait_ge(o_st[b], 8 * (g - b))
                        nc.scalar.activation(z_out[:, b, :], ps[:, BO + b, :], ACT.Copy).then_inc(o_out, 1)
                    else:
                        act.wait_ge(m_w, 2 * (g - NT) + 1)
                        nc.scalar.activation(wgt[:, b, :], nm_pair[:, b, :], ACT.Exp, bias=nm[:, b:b + 1],
                                             scale=-1.0).then_inc(m_w, 1)

                for half in range(2):
                    g0 = half * NT
                    step(g0, 0, half, True, False, False)
                    step(g0 + 1, 1, half, True, True, False)
                    for b in range(2):
                        step(g0 + 2 + b, b, half, True, True, True)
                    with act.Fori(2, NT // 2) as i:
                        for b in range(2):
                            step(g0 + 2 * i + b, b, half, True, True, True)
                    if half == 0:
                        step(g0 + NT, 0, half, False, True, True)
                        finish(g0 + NT - 1, 1, half)

                def deviation(t0, t1, k):
                    act.wait_ge(n_var, k)
                    nc.scalar.activation(std[:, t0:t1, :], std[:, t0:t1, :], ACT.Sqrt).then_inc(n_std, 1)

                def x1_group(g, b):
                    for k in range(TC):
                        n = TC * g + k
                        act.wait_ge(x1_full, n + 1)
                        nc.scalar.activation(X1[:, HI, bass.ds(n, 1), :].rearrange("p a d -> p (a d)"),
                                             z_in[:, b, k, :], ACT.Copy).then_inc(x1_hi, 1)

                turned(2 * NT - 1, 0)
                turned(2 * NT - 1, 1)
                finish(2 * NT - 2, 0, 1)
                deviation(0, NT - 2, 1)
                turned(2 * NT - 1, 2)
                turned(2 * NT - 1, 3)
                for g in range(3):
                    x1_group(g, g % 2)
                finish(2 * NT - 1, 1, 1)
                x1_group(3, 1)
                deviation(NT - 2, NT, 2)
                with act.Fori(2, NB // 2) as i:
                    for b in range(2):
                        x1_group(2 * i + b, b)
                for e in range(KD):
                    act.wait_ge(w_tr, e + 1)
                    nc.scalar.activation(WT[:, HI, e, :], ps[:, 4 + e, :], ACT.Copy).then_inc(w_hi, 1)

                def root(nb, k):
                    act.wait_ge(f_var, TC * nb + k + 1)
                    nc.scalar.activation(std2[:, k:k + 1], vare[:, k:k + 1], ACT.Sqrt).then_inc(f_std, 1)

                def rows(nb, outputs):
                    if outputs is not None:
                        for k in range(TC):
                            root(outputs, k)
                        act.wait_ge(f_mm, TC * (outputs + 1))
                    for d in range(KD):
                        act.wait_ge(g_mm, KD * nb + d + 1)
                        nc.scalar.activation(G[:, HI, d, :], ps[:, BG + d, :], ACT.Copy).then_inc(g_hi, 1)

                rows(0, None)
                with act.Fori(1, NB) as nb:
                    rows(nb, nb - 1)
                for k in range(TC):
                    root(NB - 1, k)

            @block.vector
            def _(dve):
                def x_out(G, b, j):
                    n = TC * G + j
                    dve.wait_ge(xt_hi, n + 1)
                    nc.vector.tensor_tensor(xT(b, LO)[:, :, j * P:(j + 1) * P],
                                            ps[:, BA + j % 2, :].rearrange("p (k n) -> p k n", n=P),
                                            xT(b, HI)[:, :, j * P:(j + 1) * P].bitcast(fp32),
                                            ALU.subtract).then_inc(xt_lo, 1)
                    wait(dve, c_out, n - 1)
                    nc.vector.tensor_tensor_reduce(out=xu[:, :], in0=rows[:, j, :], in1=bk_q[:, :], scale=1.0,
                                                   scalar=bqbk[:, 0:1], op0=ALU.mult, op1=ALU.add,
                                                   accum_out=c_tmp[:, j % 2:j % 2 + 1]).then_inc(c_sum, 1)

                def c_keep(n, b):
                    dve.wait_ge(c_sum, n + 1)
                    nc.vector.tensor_copy(c_all[:, bass.ds(n, 1)], c_tmp[:, b:b + 1]).then_inc(c_out, 1)

                def raw_split(weight, raw, e, count):
                    dve.wait_ge(s_whi, count)
                    nc.vector.tensor_tensor(weight[:, LO, e, :], raw[:, e, :], weight[:, HI, e, :].bitcast(fp32),
                                            ALU.subtract).then_inc(s_wlo, 1)

                for e in range(KD):
                    raw_split(wq_s, wa, e, 2 * e + 1)
                    raw_split(wk_s, wb, e, 2 * e + 2)
                dve.wait_ge(s_bc, 48)
                nc.vector.tensor_tensor(bb[:, :], bcol[:, 0, :], bcol[:, 1, :], ALU.mult).then_inc(s_bb, 1)
                dve.wait_ge(s_one, 1)
                for b in range(3):
                    dve.wait_ge(s_rhi, b + 1)
                    for e in range(KD):
                        last = nc.vector.scalar_tensor_tensor(out=brep[:, LO, b, e, :], in0=ones[:, :],
                                                              scalar=bcol[:, b, e:e + 1],
                                                              in1=brep[:, HI, b, e, :].bitcast(fp32),
                                                              op0=ALU.mult, op1=ALU.subtract)
                    last.then_inc(s_rep, 1)
                for e in range(KD):
                    raw_split(wv_s, wc, e, 2 * KD + e + 1)
                for d in range(KD):
                    dve.wait_ge(s_ahi, d + 1)
                    nc.vector.scalar_tensor_tensor(out=Aq[:, LO, d, :], in0=ps[:, d, :], scalar=SCALE,
                                                   in1=Aq[:, HI, d, :].bitcast(fp32), op0=ALU.mult,
                                                   op1=ALU.subtract).then_inc(s_alo, 1)
                dve.wait_ge(s_rmm, 3)
                nc.vector.tensor_scalar(xu[:, :], ps[:, 4, :], SCALE, None, ALU.mult).then_inc(s_rout, 1)
                nc.vector.tensor_scalar(bk_q[:, :], ps[:, 5, :], SCALE, None, ALU.mult).then_inc(s_rout, 1)
                nc.vector.tensor_scalar(bb[:, :], ps[:, 6, 0:KD], SCALE, None, ALU.mult).then_inc(s_rout, 1)
                dve.wait_ge(s_rout, 3)
                nc.vector.reduce_sum(bqbk[:, :], bb[:, :], AX.X).then_inc(s_bsum, 1)
                for e in range(KD):
                    dve.wait_ge(s_mhi, e + 1)
                    nc.vector.tensor_tensor(wmT_s[:, LO, e, :], ps[:, e, :], wmT_s[:, HI, e, :].bitcast(fp32),
                                            ALU.subtract).then_inc(s_wmc, 1)
                dve.wait_ge(s_bsum, 1)
                dve.wait_ge(s_bqt, 1)
                nc.vector.tensor_copy(bq_k[:, :, :], ps[:, 7, :].rearrange("p (k n) -> p k n", n=P)[:, :, 0:1])\
                         .then_inc(s_rout, 1)
                for j in range(2):
                    x_out(0, 0, j)
                    c_keep(j, j)
                for d in range(KD):
                    dve.wait_ge(s_vhi, d + 1)
                    nc.vector.tensor_tensor(Wvm[:, LO, d, :], ps[:, 4 + d, :], Wvm[:, HI, d, :].bitcast(fp32),
                                            ALU.subtract).then_inc(s_vlo, 1)
                    if d < 2:
                        x_out(0, 0, 2 + d)
                        c_keep(2 + d, d)
                dve.wait_ge(s_bmm, 1)
                dve.wait_ge(s_bm, 16)
                nc.vector.tensor_tensor(bias_o[:, :], ps[:, 3, :], bias_o[:, :], ALU.add).then_inc(s_bout, 1)

                def group(G, b, turn_next):
                    for e in range(KD):
                        if turn_next:
                            x_out(G + 1, 1 - b, e)
                        dve.wait_ge(t_hi, KD * G + e + 1)
                        nc.vector.scalar_tensor_tensor(out=queries(b, LO)[:, :, e * P:(e + 1) * P],
                                                       in0=ps[:, BC + e, :].rearrange("p (j n) -> p j n", n=P),
                                                       scalar=bq_k[:, e, :],
                                                       in1=queries(b, HI)[:, :, e * P:(e + 1) * P].bitcast(fp32),
                                                       op0=ALU.add, op1=ALU.subtract).then_inc(t_lo, 1)
                        if turn_next:
                            c_keep(TC * (G + 1) + e, e % 2)

                def value_out(g, tile, b):
                    dve.wait_ge(vp_hi, g + 1)
                    nc.vector.tensor_tensor(VP[:, LO, tile, :], ps[:, BC + b, :], VP[:, HI, tile, :].bitcast(fp32),
                                            ALU.subtract).then_inc(vp_lo, 1)

                def kv_chunk(section, c):
                    for j in range(TC):
                        b = j % 2
                        tile = TC * c + j
                        g = section * MT + tile
                        dve.wait_ge(k_hi, g + 1)
                        nc.vector.tensor_tensor(KT[:, LO, :, bass.ts(tile, P)],
                                                ps[:, BA + b, :].rearrange("p (k n) -> p k n", n=P),
                                                KT[:, HI, :, bass.ts(tile, P)].bitcast(fp32),
                                                ALU.subtract).then_inc(k_lo, 1)
                        dve.wait_ge(vt_hi, g + 1)
                        nc.vector.tensor_tensor(valueT[:, b, LO, :], ps[:, BB + b, :], valueT[:, b, HI, :].bitcast(fp32),
                                                ALU.subtract).then_inc(vt_lo, 1)
                        if not isinstance(tile, int) or tile > 0:
                            value_out(g - 1, tile - 1, 1 - b)
                        elif section == 1:
                            value_out(g - 1, MT - 1, 1 - b)

                group_loop(dve, group)
                for section in range(2):
                    kv_chunk(section, 0)
                    with dve.Fori(1, MC) as c:
                        kv_chunk(section, c)
                value_out(NT - 1, MT - 1, 1)

                def masked(g, b, c, i, half):
                    if c == 0:
                        dve.wait_ge(adj_in[b], 16 * (half * NT // 2 + i + 1))
                        wait(dve, p_tr, MC * (g - 1))
                        nc.vector.tensor_copy(c_now[:, b:b + 1], c_all[:, bass.ds(2 * i + b, 1)]).then_inc(s_c, 1)
                        dve.wait_ge(s_c, g + 1)
                    dve.wait_ge(s_mm, MC * g + c + 1)
                    nc.vector.scalar_tensor_tensor(out=prob[:, b, c * C:(c + 1) * C], in0=ps[:, BS + c, :],
                                                   scalar=c_now[:, b:b + 1], in1=adj_rows[:, b, c * C:(c + 1) * C],
                                                   op0=ALU.add, op1=ALU.mult).then_inc(s_adj, 1)

                def small_scores(g, b, c):
                    dve.wait_ge(s_abs, MC * g + c + 1)
                    nc.vector.tensor_scalar(small[:, c % 2, :], small[:, c % 2, :], EPS_SCORE, MASKED,
                                            ALU.is_lt, ALU.mult).then_inc(s_neg, 1)

                def small_ready(g, c):
                    dve.wait_ge(s_neg, MC * g + c + 1)

                def threshold(b, c):
                    nc.vector.tensor_tensor_reduce(out=prob[:, b, c * C:(c + 1) * C], in0=prob[:, b, c * C:(c + 1) * C],
                                                   in1=small[:, c % 2, :], scale=1.0, scalar=-3.4e38, op0=ALU.add,
                                                   op1=ALU.max, accum_out=chunk_max[:, b, c:c + 1]).then_inc(s_mask, 1)

                def maximum(g, b, n, half):
                    dve.wait_ge(s_mask, MC * (g + 1))
                    wait(dve, s_exp, g - 1)
                    nc.vector.tensor_reduce(nmax[:, b:b + 1], chunk_max[:, b, :], AX.X, ALU.max, negate=True)\
                             .then_inc(s_max, 1)

                def keep_maximum(g, b, n, half):
                    dve.wait_ge(s_max, g + 1)
                    nc.vector.tensor_copy(neg_max[:, bass.ds(n, 1), half], nmax[:, b:b + 1])

                def keep_sum(g, b, n, half):
                    dve.wait_ge(s_exp, g + 1)
                    nc.vector.tensor_copy(row_sum[:, bass.ds(n, 1), half], rsum[:, b:b + 1]).then_inc(s_keep, 1)

                def turned(g, r):
                    dve.wait_ge(p_hi, MC * g + r + 1)
                    nc.vector.tensor_tensor(probT[:, r % 2, LO, :], ps[:, BP + r % 2, :],
                                            probT[:, r % 2, HI, :].bitcast(fp32), ALU.subtract).then_inc(p_lo, 1)

                def pick(g, b, n):
                    k = g - NT
                    nc.vector.tensor_copy(nm_pair[:, b, :], neg_max[:, bass.ds(n, 1), :].rearrange("p a h -> p (a h)"))
                    nc.vector.tensor_copy(ls_pair[:, b, :], row_sum[:, bass.ds(n, 1), :].rearrange("p a h -> p (a h)"))\
                             .then_inc(m_step, 1)
                    dve.wait_ge(m_step, 7 * k + 1)
                    nc.vector.tensor_reduce(nm[:, b:b + 1], nm_pair[:, b, :], AX.X, ALU.min).then_inc(m_w, 1)

                def merge(g, b, i):
                    k = g - NT
                    dve.wait_ge(m_w, 2 * k + 2)
                    nc.vector.tensor_tensor(wls[:, b, :], wgt[:, b, :], ls_pair[:, b, :], ALU.mult).then_inc(m_step, 1)
                    dve.wait_ge(m_step, 7 * k + 2)
                    nc.vector.reduce_sum(den[:, b:b + 1], wls[:, b, :], AX.X).then_inc(m_step, 1)
                    dve.wait_ge(m_step, 7 * k + 3)
                    nc.vector.reciprocal(rden[:, b:b + 1], den[:, b:b + 1]).then_inc(m_step, 1)
                    dve.wait_ge(m_step, 7 * k + 4)
                    nc.vector.tensor_scalar(wn[:, b, :], wgt[:, b, :], rden[:, b:b + 1], None, ALU.mult).then_inc(m_step, 1)
                    dve.wait_ge(xo_in[b], 32 * (i + 1))
                    dve.wait_ge(o_st[b], 16 * (NT // 2 + i))
                    nc.vector.tensor_tensor(x_in[:, b, :], x_in[:, b, :], bias_o[:, :], ALU.add).then_inc(xb, 1)
                    dve.wait_ge(m_step, 7 * k + 5)
                    dve.wait_ge(xb, k + 1)
                    nc.vector.scalar_tensor_tensor(out=x_in[:, b, :], in0=o_in[:, b, :], scalar=wn[:, b, 0:1],
                                                   in1=x_in[:, b, :], op0=ALU.mult, op1=ALU.add).then_inc(m_step, 1)
                    dve.wait_ge(o_mm, g + 1)
                    dve.wait_ge(m_step, 7 * k + 6)
                    nc.vector.scalar_tensor_tensor(out=z_out[:, b, :], in0=ps[:, BO + b, :], scalar=wn[:, b, 1:2],
                                                   in1=x_in[:, b, :], op0=ALU.mult, op1=ALU.add).then_inc(o_out, 1)
                    dve.wait_ge(o_out, g + 1)
                    nc.vector.bn_stats(bst[:, b, :], z_out[:, b, :]).then_inc(m_step, 1)

                def row_stats(g, b, n):
                    k = g - NT
                    nc.vector.bn_aggr(mv[:, b, :], bst[:, b, :]).then_inc(s_mv, 1)
                    dve.wait_ge(s_mv, k + 1)
                    nc.vector.tensor_copy(stats[:, bass.ds(n, 1), :].rearrange("p a h -> p (a h)"), mv[:, b, :])\
                             .then_inc(s_stat, 1)

                def step(g, b, i, half, make, use, fin):
                    n = None if i is None else 2 * i + b
                    fin = fin and half == 1
                    if use:
                        keep_sum(g - 1, 1 - b, (NT if n is None else n) - 1, half)
                    if fin:
                        pick(g - 2, b, (NT if n is None else n) - 2)
                    if make:
                        masked(g, b, 0, i, half)
                        masked(g, b, 1, i, half)
                        small_scores(g, b, 0)
                        small_ready(g, 0)
                    if use:
                        turned(g - 1, 0)
                    if make:
                        threshold(b, 0)
                    if make:
                        masked(g, b, 2, i, half)
                        small_scores(g, b, 1)
                        small_ready(g, 1)
                    if use:
                        turned(g - 1, 1)
                    if make:
                        threshold(b, 1)
                        masked(g, b, 3, i, half)
                        small_scores(g, b, 2)
                        small_ready(g, 2)
                        small_scores(g, b, 3)
                        threshold(b, 2)
                        small_ready(g, 3)
                    if use:
                        turned(g - 1, 2)
                    if make:
                        threshold(b, 3)
                        maximum(g, b, n, half)
                    if use:
                        turned(g - 1, 3)
                    if fin:
                        merge(g - 2, b, (NT // 2 if i is None else i) - 1)
                        dve.wait_ge(m_step, 7 * (g - 2 - NT) + 7)
                    if make:
                        keep_maximum(g, b, n, half)
                    if fin:
                        row_stats(g - 2, b, (NT if n is None else n) - 2)

                for half in range(2):
                    g0 = half * NT
                    step(g0, 0, 0, half, True, False, False)
                    step(g0 + 1, 1, 0, half, True, True, False)
                    for b in range(2):
                        step(g0 + 2 + b, b, 1, half, True, True, True)
                    with dve.Fori(2, NT // 2) as i:
                        for b in range(2):
                            step(g0 + 2 * i + b, b, i, half, True, True, True)
                    if half == 0:
                        step(g0 + NT, 0, None, half, False, True, True)

                def variances(t0, t1):
                    dve.wait_ge(s_stat, t1)
                    nc.vector.tensor_scalar(std[:, t0:t1, :], stats[:, t0:t1, 1:2], EPS_LN, None, ALU.add).then_inc(n_var, 1)

                def deviations(t0, t1, k):
                    dve.wait_ge(n_std, k)
                    nc.vector.reciprocal(rstd[:, t0:t1, :], std[:, t0:t1, :]).then_inc(n_rstd, 1)
                    dve.wait_ge(n_rstd, k)

                def x1_group(i, b):
                    def low(k):
                        n = TC * (2 * i + b) + k
                        dve.wait_ge(x1_hi, n + 1)
                        nc.vector.tensor_tensor(X1[:, LO, bass.ds(n, 1), :].rearrange("p a d -> p (a d)"),
                                                z_in[:, b, k, :],
                                                X1[:, HI, bass.ds(n, 1), :].rearrange("p a d -> p (a d)"),
                                                ALU.subtract).then_inc(x1_lo, 1)

                    dve.wait_ge(zg_in[b], 16 * (i + 1))
                    for k in range(TC):
                        n = TC * (2 * i + b) + k
                        nc.vector.tensor_scalar(z_in[:, b, k, :], z_in[:, b, k, :], stats[:, bass.ds(n, 1), 0],
                                                rstd[:, bass.ds(n, 1), 0], ALU.subtract, ALU.mult).then_inc(x1_full, 1)
                        if k > 0:
                            low(k - 1)
                    low(TC - 1)

                keep_sum(2 * NT - 1, 1, NT - 1, 1)
                pick(2 * NT - 2, 0, NT - 2)
                variances(0, NT - 2)
                for r in range(MC):
                    turned(2 * NT - 1, r)
                deviations(0, NT - 2, 1)
                for b in range(2):
                    x1_group(0, b)
                for b in range(2):
                    g, n = 2 * NT - 2 + b, NT - 2 + b
                    if b == 1:
                        pick(g, b, n)
                    merge(g, b, NT // 2 - 1)
                    dve.wait_ge(m_step, 7 * (n + 1))
                    row_stats(g, b, n)
                    x1_group(1, b)
                variances(NT - 2, NT)
                deviations(NT - 2, NT, 2)
                with dve.Fori(2, NB // 2) as i:
                    for b in range(2):
                        x1_group(i, b)
                for e in range(KD):
                    dve.wait_ge(w_hi, e + 1)
                    nc.vector.tensor_tensor(WT[:, LO, e, :], ps[:, 4 + e, :], WT[:, HI, e, :].bitcast(fp32),
                                            ALU.subtract).then_inc(w_lo, 1)

                def normalised(nb, k):
                    t = TC * nb + k
                    dve.wait_ge(zf_in[k], 16 * (nb + 1))
                    nc.vector.tensor_scalar(zf[:, k, :], zf[:, k, :], stats[:, bass.ds(t, 1), 0],
                                            rstd[:, bass.ds(t, 1), 0], ALU.subtract, ALU.mult).then_inc(f_x1, 1)

                def second_layer(nb, k):
                    t = TC * nb + k
                    dve.wait_ge(f_mm, t + 1)
                    nc.vector.tensor_tensor(y[:, k, :], ps[:, BF + k % 2, :], b1_rep[:, :], ALU.add).then_inc(f_out, 1)
                    dve.wait_ge(f_x1, t + 1)
                    dve.wait_ge(f_out, t + 1)
                    nc.vector.scalar_tensor_tensor(out=y[:, k, :], in0=y[:, k, :], scalar=0.0, in1=zf[:, k, :],
                                                   op0=ALU.max, op1=ALU.add).then_inc(f_sum, 1)
                    dve.wait_ge(f_sum, t + 1)
                    nc.vector.bn_stats(bst2[:, k, :], y[:, k, :]).then_inc(f_bn, 1)
                    dve.wait_ge(f_bn, t + 1)

                def variance(nb, k):
                    t = TC * nb + k
                    nc.vector.bn_aggr(mv2[:, k, :], bst2[:, k, :]).then_inc(f_mv, 1)
                    dve.wait_ge(f_mv, t + 1)
                    nc.vector.tensor_scalar(vare[:, k:k + 1], mv2[:, k, 1:2], EPS_LN, None, ALU.add).then_inc(f_var, 1)

                def result(nb, k):
                    t = TC * nb + k
                    dve.wait_ge(f_std, t + 1)
                    nc.vector.reciprocal(rstd2[:, k:k + 1], std2[:, k:k + 1]).then_inc(f_rstd, 1)
                    dve.wait_ge(f_rstd, t + 1)
                    wait(dve, out_st[k], 16 * nb)
                    nc.vector.tensor_scalar(res[:, k, :], y[:, k, :], mv2[:, k, 0:1], rstd2[:, k:k + 1],
                                            ALU.subtract, ALU.mult).then_inc(f_res, 1)

                def outputs(nb):
                    for k in range(TC - 1):
                        normalised(nb, k)
                    second_layer(nb, 0)
                    normalised(nb, TC - 1)
                    variance(nb, 0)
                    for k in range(1, TC):
                        second_layer(nb, k)
                        result(nb, k - 1)
                        variance(nb, k)
                    result(nb, TC - 1)

                def g_split(nb):
                    for d in range(KD):
                        dve.wait_ge(g_hi, KD * nb + d + 1)
                        nc.vector.tensor_tensor(G[:, LO, d, :], ps[:, BG + d, :], G[:, HI, d, :].bitcast(fp32),
                                                ALU.subtract).then_inc(g_lo, 1)

                dve.wait_ge(b1_in, 16)
                g_split(0)
                outputs(0)
                g_split(1)
                with dve.Fori(2, NB) as nb:
                    outputs(nb - 1)
                    g_split(nb)
                outputs(NB - 1)


_INS = ["x", "adj", "L0_gnn_key", "L0_gnn_value", "L0_gnn_Wq", "L0_gnn_bq", "L0_gnn_Wk", "L0_gnn_bk", "L0_gnn_Wv",
        "L0_gnn_bv", "L0_gnn_Wm", "L0_gnn_bm", "L1_gnn_W", "L1_gnn_b"]


def kernel(**inputs):
    import numpy as _np
    import concourse.bacc as _bacc
    from concourse.bass_utils import run_bass_kernel_spmd as _run

    nc = _bacc.Bacc("TRN2", target_bir_lowering=False, num_devices=1)
    arrays, args = {}, []
    for name in _INS:
        a = _np.ascontiguousarray(inputs[name])
        arrays["in_" + name] = a
        args.append(nc.dram_tensor("in_" + name, a.shape, mybir.dt.from_np(a.dtype), kind="ExternalInput").ap())
    args.append(nc.dram_tensor("out_0", (4096, 512), fp32, kind="ExternalOutput").ap())
    attention_then_aggregation(nc, *args)
    r = _run(nc, [arrays], core_ids=[0])
    return r.results[0]["out_0"]
```
